# Optimizing a Trainium2 kernel written in Bass

```python
import numpy as np
import jax
import jax.numpy as jnp

def _softmax(x, axis=-1):
    return jax.nn.softmax(x, axis=axis)
def _gelu(x):
    return jax.nn.gelu(x, approximate=True)
def _silu(x):
    return jax.nn.silu(x)
def _sigmoid(x):
    return jax.nn.sigmoid(x)
def _layernorm(x, axis=-1, eps=1e-5):
    m = jnp.mean(x, axis=axis, keepdims=True)
    v = jnp.var(x, axis=axis, keepdims=True)
    return (x - m) / jnp.sqrt(v + eps)
def _scatter_add(tgt, idx, src, axis=0):
    return tgt.at[idx].add(src)
def _segment_sum(src, seg, n):
    return jax.ops.segment_sum(src, seg, n)

kernel_name = 'mk_conv_attn_hybrid_d2_conv_nchw128_38bfab'

def setup_inputs(seed: int = 0):
    np.random.seed(seed)
    _w = jnp.asarray
    def _rec_inputs():
        import jax
        import jax.numpy as jnp
        _gk = jax.random.key(seed)
        x = -0.0002928 + 1 * jax.random.normal(jax.random.fold_in(_gk, 1), (32, 128, 32, 32), jnp.float32)
        return x
    x = _rec_inputs()
    def _L0_conv_setup():
        import jax, jax.numpy as jnp
        import numpy as np
        BN_EPS = 1e-05

        def tanhshrink(x):
            return x - jnp.tanh(x)
        key = jax.random.key(seed)
        ks = jax.random.split(key, 10)
        B, C, H, W = (32, 128, 32, 32)
        RIN, RH, OC = (256, 512, 128)
        s = lambda k, shape, fan: jax.random.normal(k, shape, dtype=jnp.float32) * (1.0 / np.sqrt(fan))
        return {'x': jax.random.normal(ks[0], (B, C, H, W), dtype=jnp.float32), 'gamma': jnp.ones((C,), jnp.float32), 'beta': jnp.zeros((C,), jnp.float32), 'w_in': s(ks[1], (RIN, C), C), 'b_in': jnp.zeros((RIN,), jnp.float32), 'w_ih': s(ks[2], (RH, RIN), RIN), 'b_ih': jnp.zeros((RH,), jnp.float32), 'w_hh': s(ks[3], (RH, RH), RH), 'b_hh': jnp.zeros((RH,), jnp.float32), 'w_out': s(ks[4], (OC, RH), RH), 'b_out': jnp.zeros((OC,), jnp.float32)}
    _L0_conv_all = _L0_conv_setup()
    _L0_conv_in = {k: v for k, v in _L0_conv_all.items() if k in ('gamma', 'beta', 'w_in', 'b_in', 'w_ih', 'b_ih', 'w_hh', 'b_hh', 'w_out', 'b_out', )}
    del _L0_conv_all

    def _L1_attn_setup():
        import jax, jax.numpy as jnp
        import numpy as np
        from jax import lax
        TAU_MEM = 10.0
        THRESHOLD = 1.0
        WINDOW = 128
        STRIDE = 64
        NUM_GLOBAL = 4

        def _spike_indicators(x, Ws, bs):
            B, S, D = x.shape
            decay = jnp.exp(jnp.float32(-1.0 / TAU_MEM))
            cur = x @ Ws + bs
            cur_t = jnp.swapaxes(cur, 0, 1)

            def step(mem, c):
                mem = decay * mem + c
                spk = mem >= THRESHOLD
                mem = jnp.where(spk, 0.0, mem)
                return (mem, spk.astype(jnp.float32))
            _, spikes = lax.scan(step, jnp.zeros((B, 1), jnp.float32), cur_t)
            spike_ind = spikes.mean(axis=1)[:, 0]
            return spike_ind != 0.0

        def _sparse_mask(S, spike_bool):
            i = jnp.arange(S)[:, None]
            j = jnp.arange(S)[None, :]
            local = (j <= i) & (j >= i - WINDOW)
            glob = j % STRIDE == 0
            first = j < NUM_GLOBAL
            return (local | glob | first) & spike_bool[None, :]
        key = jax.random.key(seed)
        ks = jax.random.split(key, 8)
        B, S, D = (2, 8192, 128)
        s = 1.0 / np.sqrt(D)
        x = jax.random.normal(ks[0], (B, S, D), jnp.float32)
        Wq = jax.random.normal(ks[1], (D, D), jnp.float32) * s
        Wk = jax.random.normal(ks[2], (D, D), jnp.float32) * s
        Wv = jax.random.normal(ks[3], (D, D), jnp.float32) * s
        Wo = jax.random.normal(ks[4], (D, D), jnp.float32) * s
        Ws = jax.random.normal(ks[5], (D, 1), jnp.float32) * s
        return {'x': x, 'Wq': Wq, 'bq': jnp.zeros((D,), jnp.float32), 'Wk': Wk, 'bk': jnp.zeros((D,), jnp.float32), 'Wv': Wv, 'bv': jnp.zeros((D,), jnp.float32), 'Wo': Wo, 'bo': jnp.zeros((D,), jnp.float32), 'Ws': Ws, 'bs': jnp.zeros((1,), jnp.float32)}
    _L1_attn_all = _L1_attn_setup()
    _L1_attn_in = {k: v for k, v in _L1_attn_all.items() if k in ('Wq', 'bq', 'Wk', 'bk', 'Wv', 'bv', 'Wo', 'bo', 'Ws', 'bs', )}
    del _L1_attn_all

    def _L1_ffn_setup():
        import jax, jax.numpy as jnp
        import numpy as np
        B, S, D, E, H, O, K = (512, 2048, 128, 64, 512, 128, 8)
        key = jax.random.key(seed)
        k0, k1, k2, k3 = jax.random.split(key, 4)
        x = jax.random.normal(k0, (B, S, D), dtype=jnp.float32)
        gate_w = jax.random.normal(k1, (E, D), dtype=jnp.float32) * (1.0 / np.sqrt(D))
        gate_b = jnp.zeros((E,), dtype=jnp.float32)
        weight1 = jax.random.uniform(k2, (E, D + 1, H), dtype=jnp.float32, minval=-1.0, maxval=1.0) * (1.0 / np.sqrt(D + 1))
        weight2 = jax.random.uniform(k3, (E, H + 1, O), dtype=jnp.float32, minval=-1.0, maxval=1.0) * (1.0 / np.sqrt(H + 1))
        return {'x': x, 'gate_w': gate_w, 'gate_b': gate_b, 'weight1': weight1, 'weight2': weight2}
    _L1_ffn_all = _L1_ffn_setup()
    _L1_ffn_in = {k: v for k, v in _L1_ffn_all.items() if k in ('gate_w', 'gate_b', 'weight1', 'weight2', )}
    del _L1_ffn_all

    return {
        "x": x,
        "L0_conv_gamma": _L0_conv_in["gamma"],
        "L0_conv_beta": _L0_conv_in["beta"],
        "L0_conv_w_in": _L0_conv_in["w_in"],
        "L0_conv_b_in": _L0_conv_in["b_in"],
        "L0_conv_w_ih": _L0_conv_in["w_ih"],
        "L0_conv_b_ih": _L0_conv_in["b_ih"],
        "L0_conv_w_hh": _L0_conv_in["w_hh"],
        "L0_conv_b_hh": _L0_conv_in["b_hh"],
        "L0_conv_w_out": _L0_conv_in["w_out"],
        "L0_conv_b_out": _L0_conv_in["b_out"],
        "L1_attn_Wq": _L1_attn_in["Wq"],
        "L1_attn_bq": _L1_attn_in["bq"],
        "L1_attn_Wk": _L1_attn_in["Wk"],
        "L1_attn_bk": _L1_attn_in["bk"],
        "L1_attn_Wv": _L1_attn_in["Wv"],
        "L1_attn_bv": _L1_attn_in["bv"],
        "L1_attn_Wo": _L1_attn_in["Wo"],
        "L1_attn_bo": _L1_attn_in["bo"],
        "L1_attn_Ws": _L1_attn_in["Ws"],
        "L1_attn_bs": _L1_attn_in["bs"],
        "L1_ffn_gate_w": _L1_ffn_in["gate_w"],
        "L1_ffn_gate_b": _L1_ffn_in["gate_b"],
        "L1_ffn_weight1": _L1_ffn_in["weight1"],
        "L1_ffn_weight2": _L1_ffn_in["weight2"],
    }

def reference(x, L0_conv_gamma, L0_conv_beta, L0_conv_w_in, L0_conv_b_in, L0_conv_w_ih, L0_conv_b_ih, L0_conv_w_hh, L0_conv_b_hh, L0_conv_w_out, L0_conv_b_out, L1_attn_Wq, L1_attn_bq, L1_attn_Wk, L1_attn_bk, L1_attn_Wv, L1_attn_bv, L1_attn_Wo, L1_attn_bo, L1_attn_Ws, L1_attn_bs, L1_ffn_gate_w, L1_ffn_gate_b, L1_ffn_weight1, L1_ffn_weight2):
    import jax
    import jax.numpy as jnp
    def _L0_conv_ref(x, gamma, beta, w_in, b_in, w_ih, b_ih, w_hh, b_hh, w_out, b_out):
        import jax, jax.numpy as jnp
        import numpy as np
        BN_EPS = 1e-05

        def tanhshrink(x):
            return x - jnp.tanh(x)
        B, C, H, W = x.shape
        RH = w_hh.shape[0]
        mean = jnp.mean(x, axis=(0, 2, 3), keepdims=True)
        var = jnp.var(x, axis=(0, 2, 3), keepdims=True)
        xn = (x - mean) * jax.lax.rsqrt(var + BN_EPS)
        xn = xn * gamma[None, :, None, None] + beta[None, :, None, None]
        seq = jnp.transpose(xn, (0, 2, 3, 1)).reshape(B, H * W, C)
        inp = tanhshrink(jnp.einsum('blc,ic->bli', seq, w_in) + b_in)
        xgate = jnp.einsum('bli,hi->blh', inp, w_ih) + b_ih + b_hh
        xgate_t = jnp.transpose(xgate, (1, 0, 2))

        def step(h, xg):
            h_new = jnp.tanh(xg + h @ w_hh.T)
            return (h_new, h_new)
        h0 = jnp.zeros((B, RH), x.dtype)
        _, hs = jax.lax.scan(step, h0, xgate_t)
        outputs = jnp.transpose(hs, (1, 0, 2))
        out_seq = jnp.einsum('blh,oh->blo', outputs, w_out) + b_out
        out = jnp.transpose(out_seq.reshape(B, H, W, -1), (0, 3, 1, 2))
        return out

    def _L1_attn_ref(x, Wq, bq, Wk, bk, Wv, bv, Wo, bo, Ws, bs):
        import jax, jax.numpy as jnp
        import numpy as np
        from jax import lax
        TAU_MEM = 10.0
        THRESHOLD = 1.0
        WINDOW = 128
        STRIDE = 64
        NUM_GLOBAL = 4

        def _spike_indicators(x, Ws, bs):
            B, S, D = x.shape
            decay = jnp.exp(jnp.float32(-1.0 / TAU_MEM))
            cur = x @ Ws + bs
            cur_t = jnp.swapaxes(cur, 0, 1)

            def step(mem, c):
                mem = decay * mem + c
                spk = mem >= THRESHOLD
                mem = jnp.where(spk, 0.0, mem)
                return (mem, spk.astype(jnp.float32))
            _, spikes = lax.scan(step, jnp.zeros((B, 1), jnp.float32), cur_t)
            spike_ind = spikes.mean(axis=1)[:, 0]
            return spike_ind != 0.0

        def _sparse_mask(S, spike_bool):
            i = jnp.arange(S)[:, None]
            j = jnp.arange(S)[None, :]
            local = (j <= i) & (j >= i - WINDOW)
            glob = j % STRIDE == 0
            first = j < NUM_GLOBAL
            return (local | glob | first) & spike_bool[None, :]
        B, S, D = x.shape
        spike_bool = _spike_indicators(x, Ws, bs)
        mask = _sparse_mask(S, spike_bool)
        Q = x @ Wq + bq
        K = x @ Wk + bk
        V = x @ Wv + bv
        scale = jnp.float32(1.0 / np.sqrt(D))
        scores = jnp.einsum('bid,bjd->bij', Q, K) * scale
        scores = jnp.where(mask[None, :, :], scores, -jnp.inf)
        w = jax.nn.softmax(scores, axis=-1)
        w = jnp.nan_to_num(w, nan=0.0)
        out = jnp.einsum('bij,bjd->bid', w, V)
        return out @ Wo + bo

    def _L1_ffn_ref(x, gate_w, gate_b, weight1, weight2):
        import jax, jax.numpy as jnp
        import numpy as np
        B, S, D, E, H, O, K = (512, 2048, 128, 64, 512, 128, 8)
        Bn, Sn, Dn = x.shape
        logits = jnp.einsum('bsd,ed->bse', x, gate_w) + gate_b
        probs = jax.nn.softmax(logits, axis=1)
        vals, idx = jax.lax.top_k(probs.transpose(0, 2, 1), K)
        topv = vals.transpose(0, 2, 1)
        topi = idx.transpose(0, 2, 1)
        flat_idx = topi.reshape(Bn, K * E)
        gathered = jnp.take_along_axis(x, flat_idx[:, :, None], axis=1)
        gathered = gathered.reshape(Bn, K, E, Dn)
        pooled = jnp.einsum('bked,bke->bed', gathered, topv)
        ones = jnp.ones((E, Bn, 1), dtype=x.dtype)
        h = jnp.concatenate([pooled.transpose(1, 0, 2), ones], axis=-1)
        h = jax.nn.gelu(jnp.einsum('ebd,edh->ebh', h, weight1), approximate=False)
        h = jnp.concatenate([h, ones], axis=-1)
        out = jnp.einsum('ebh,eho->ebo', h, weight2)
        out = out.transpose(1, 0, 2)
        weighted = jnp.einsum('beo,bke->bkeo', out, topv).reshape(Bn, K * E, O)
        outputs = jnp.zeros((Bn, Sn, O), dtype=x.dtype)
        outputs = outputs.at[jnp.arange(Bn)[:, None], flat_idx].add(weighted)
        return outputs

    def _gn(v, G=32, eps=1e-5):
        B_, C_, H_, W_ = v.shape
        g = v.reshape(B_, G, C_ // G, H_, W_)
        m = jnp.mean(g, axis=(2, 3, 4), keepdims=True)
        s = jnp.var(g, axis=(2, 3, 4), keepdims=True)
        return ((g - m) / jnp.sqrt(s + eps)).reshape(v.shape)

    def _ln_c(v, eps=1e-6):
        m = jnp.mean(v, axis=1, keepdims=True)
        s = jnp.var(v, axis=1, keepdims=True)
        return (v - m) / jnp.sqrt(s + eps)

    def _ln_t(v, eps=1e-5):
        m = jnp.mean(v, axis=-1, keepdims=True)
        s = jnp.var(v, axis=-1, keepdims=True)
        return (v - m) / jnp.sqrt(s + eps)

    def _to_tokens(v):
        B_, C_, H_, W_ = v.shape
        return v.reshape(B_, C_, H_ * W_).transpose(0, 2, 1)
    def _from_tokens(t, like):
        B_, C_, H_, W_ = like.shape
        return t.transpose(0, 2, 1).reshape(B_, C_, H_, W_)

    x = x + _L0_conv_ref(_gn(x), L0_conv_gamma, L0_conv_beta, L0_conv_w_in, L0_conv_b_in, L0_conv_w_ih, L0_conv_b_ih, L0_conv_w_hh, L0_conv_b_hh, L0_conv_w_out, L0_conv_b_out)
    t = _to_tokens(x)
    t = t + _L1_attn_ref(_ln_t(t), L1_attn_Wq, L1_attn_bq, L1_attn_Wk, L1_attn_bk, L1_attn_Wv, L1_attn_bv, L1_attn_Wo, L1_attn_bo, L1_attn_Ws, L1_attn_bs)
    t = t + _L1_ffn_ref(_ln_t(t), L1_ffn_gate_w, L1_ffn_gate_b, L1_ffn_weight1, L1_ffn_weight2)
    x = _from_tokens(t, x)
    return x


_drawn_inputs = setup_inputs


def setup_inputs(seed=0):
    import zlib

    import numpy as np

    out = dict(_drawn_inputs(seed))
    spreads = {'L0_conv_gamma': (1.0, 0.2),
     'L0_conv_beta': (0.0, 0.1),
     'L0_conv_b_in': (0.0, 0.1),
     'L0_conv_b_ih': (0.0, 0.1),
     'L0_conv_b_hh': (0.0, 0.1),
     'L0_conv_b_out': (0.0, 0.1),
     'L1_attn_bq': (0.0, 0.563),
     'L1_attn_bk': (0.0, 0.8),
     'L1_attn_bv': (0.0, 0.1),
     'L1_attn_bo': (0.0, 0.1),
     'L1_ffn_gate_b': (0.0, 0.1)}
    factors = {'L1_ffn_gate_w': 8.0, 'L1_ffn_weight1': 8.0, 'L1_ffn_weight2': 8.0}
    for name, (base, spread) in spreads.items():
        noise = np.random.default_rng([zlib.crc32(name.encode()), seed]).standard_normal(out[name].shape)
        drawn = base * np.exp(spread * noise) if base else spread * noise
        out[name] = jnp.asarray(drawn.astype(out[name].dtype))
    for name, factor in factors.items():
        out[name] = (out[name] * factor).astype(out[name].dtype)
    return out
```

```python
from contextlib import ExitStack

import concourse.bass as bass
from concourse import mybir
from concourse.alu_op_type import AluOpType as ALU

F32 = mybir.dt.float32
F16 = mybir.dt.float16
I32 = mybir.dt.int32
ACT = mybir.ActivationFunctionType
AX_X = mybir.AxisListType.X

B, C, L = 32, 128, 1024
GROUPS = 32
RIN, RH = 256, 512
KI, KH = RIN // 128, RH // 128
T = 8
NBLK = L // T
E, H, TOPK = 64, 512, 8
KE = H // 128
Q = 128
NQ = L // Q
WINDOW, STRIDE, FIRST = 128, 64, 4
NG = FIRST + L // STRIDE - 1
W_TOP = 2.0 ** 14
LO_SCALE = 2.0 ** 12
NEG = -1.0e30
DECAY = 0.9048374180359595
SCALE = 1.0 / C ** 0.5
ACT_ID = ACT.Identity


class Chain:

    def __init__(self, eng, sem, base=0):
        self.eng, self.sem, self.base, self.n = eng, sem, base, 0

    def step(self, ins):
        self.n += 1
        ins.then_inc(self.sem, 1)
        self.eng.wait_ge(self.sem, self.base + self.n)


class Store:

    def __init__(self, nc, ctx):
        self.nc, self.ctx = nc, ctx

    def sb(self, name, shape, dt=F32):
        t = self.ctx.enter_context(self.nc.sbuf_tensor(name, shape, dt))
        return t

    def ps(self, name, shape, dt=F32):
        return self.ctx.enter_context(self.nc.psum_tensor(name, shape, dt))

    def sem(self, name):
        return self.ctx.enter_context(self.nc.semaphore(name))


def load_and_norm(nc, d, x_sb, scale_cb, shift_cb):
    NLOAD = 8
    PER = B // NLOAD
    with ExitStack() as ctx:
        st = Store(nc, ctx)
        stats = st.sb("stats", [C, B, 2, 6])
        moments = st.sb("moments", [C, 2, B])
        mv = st.sb("mv", [C, B, 2])
        group_mean = st.sb("group_mean", [C, C])
        gn = st.sb("gn", [C, 2, B])
        t1 = st.sb("t1", [C, B])
        t2 = st.sb("t2", [C, B])
        gr = st.sb("gr", [C, B])
        vm = st.sb("vm", [C, B])
        e2 = st.sb("e2", [C, B])
        bn = st.sb("bn", [C, 8])
        gamma = st.sb("gamma", [C, 1])
        beta = st.sb("beta", [C, 1])
        half_neg = st.sb("half_neg", [C, B])
        ps_gn = st.ps("ps_gn", [C, 2, B])
        x_loaded = [st.sem(f"x_loaded{i}") for i in range(NLOAD)]
        params_loaded = st.sem("params_loaded")
        dve_step = st.sem("dve_step")
        stats_done = st.sem("stats_done")
        moments_ready = st.sem("moments_ready")
        group_ready = st.sem("group_ready")
        var_ready = st.sem("var_ready")
        rstd_ready = st.sem("rstd_ready")
        pow_ready = st.sem("pow_ready")
        xd = d["x"]

        with nc.Block() as block:
            @block.sync
            def _(sp):
                sp.dma_start(group_mean[:], d["c_group_mean"]).then_inc(params_loaded, 16)
                sp.dma_start(gamma[:], d["L0_conv_gamma"]).then_inc(params_loaded, 16)
                sp.dma_start(beta[:], d["L0_conv_beta"]).then_inc(params_loaded, 16)
                for i in range(NLOAD):
                    sp.dma_start(x_sb[:, i * PER:(i + 1) * PER, :],
                                 xd[i * PER:(i + 1) * PER].rearrange("b c l -> c b l")).then_inc(x_loaded[i], 16)

            @block.tensor
            def _(pe):
                pe.wait_ge(params_loaded, 48)
                pe.wait_ge(moments_ready, 2)
                nc.tensor.matmul(ps_gn[:].rearrange("p a b -> p (a b)"), group_mean[:],
                                 moments[:].rearrange("p a b -> p (a b)")).then_inc(group_ready, 1)

            @block.gpsimd
            def _(pool):
                nc.gpsimd.memset(half_neg[:], -0.5).then_inc(pow_ready, 1)
                pool.wait_ge(pow_ready, 1)
                pool.wait_ge(var_ready, 1)
                nc.gpsimd.tensor_tensor(gr[:], t2[:], half_neg[:], ALU.pow).then_inc(rstd_ready, 1)
                pool.wait_ge(var_ready, 2)
                nc.gpsimd.tensor_tensor(bn[:, 3:4], bn[:, 2:3], half_neg[:, 0:1], ALU.pow).then_inc(rstd_ready, 1)

            @block.vector
            def _(dve):
                v = nc.vector
                for i in range(NLOAD):
                    dve.wait_ge(x_loaded[i], 16)
                    with dve.Fori(i * PER, (i + 1) * PER) as b:
                        for h in range(2):
                            v.bn_stats(stats[:, bass.ds(b, 1), h, :].rearrange("p b s -> p (b s)"),
                                       x_sb[:, bass.ds(b, 1), h * 512:(h + 1) * 512].rearrange("p b l -> p (b l)")
                                       ).then_inc(stats_done, 1)
                dve.wait_ge(stats_done, 2 * B)
                for b in range(B):
                    last = v.bn_aggr(mv[:, b, :], stats[:, b])
                    last.then_inc(stats_done, 1)
                dve.wait_ge(stats_done, 3 * B)
                ch = Chain(dve, dve_step)
                v.tensor_copy(moments[:, 0, :], mv[:, :, 0]).then_inc(moments_ready, 1)
                ch.step(v.tensor_tensor(t1[:], mv[:, :, 0], mv[:, :, 0], ALU.mult))
                v.tensor_tensor(moments[:, 1, :], t1[:], mv[:, :, 1], ALU.add).then_inc(moments_ready, 1)
                dve.wait_ge(group_ready, 1)
                ch.step(v.tensor_copy(gn[:], ps_gn[:]))
                ch.step(v.tensor_tensor(t1[:], gn[:, 0, :], gn[:, 0, :], ALU.mult))
                ch.step(v.tensor_tensor(t1[:], gn[:, 1, :], t1[:], ALU.subtract))
                v.tensor_scalar(t2[:], t1[:], 1e-5, None, ALU.add).then_inc(var_ready, 1)
                dve.wait_ge(rstd_ready, 1)
                ch.step(v.tensor_tensor(t1[:], mv[:, :, 0], gn[:, 0, :], ALU.subtract))
                ch.step(v.tensor_tensor(vm[:], t1[:], gr[:], ALU.mult))
                ch.step(v.tensor_tensor(t1[:], gr[:], gr[:], ALU.mult))
                ch.step(v.tensor_tensor(t1[:], t1[:], mv[:, :, 1], ALU.mult))
                ch.step(v.tensor_reduce(bn[:, 0:1], vm[:], AX_X, ALU.add))
                ch.step(v.tensor_scalar(bn[:, 1:2], bn[:, 0:1], 1.0 / B, None, ALU.mult))
                ch.step(v.tensor_scalar(t2[:], vm[:], bn[:, 1:2], None, ALU.subtract))
                ch.step(v.tensor_tensor(t2[:], t2[:], t2[:], ALU.mult))
                ch.step(v.tensor_tensor(e2[:], t1[:], t2[:], ALU.add))
                ch.step(v.tensor_reduce(bn[:, 4:5], e2[:], AX_X, ALU.add))
                v.tensor_scalar(bn[:, 2:3], bn[:, 4:5], 1.0 / B, 1e-5, ALU.mult, ALU.add).then_inc(var_ready, 1)
                dve.wait_ge(rstd_ready, 2)
                dve.wait_ge(params_loaded, 48)
                ch.step(v.tensor_tensor(bn[:, 5:6], bn[:, 3:4], gamma[:], ALU.mult))
                ch.step(v.tensor_scalar(scale_cb[:], gr[:], bn[:, 5:6], None, ALU.mult))
                ch.step(v.tensor_tensor(t1[:], gn[:, 0, :], gr[:], ALU.mult))
                ch.step(v.tensor_scalar(t1[:], t1[:], bn[:, 1:2], bn[:, 5:6], ALU.add, ALU.mult))
                ch.step(v.tensor_scalar(shift_cb[:], t1[:], -1.0, beta[:, 0:1], ALU.mult, ALU.add))


def rnn_layer(nc, d, x_sb, scale_cb, shift_cb, ln_r, ln_mr, spikes):
    with ExitStack() as ctx:
        st = Store(nc, ctx)
        w_in = st.sb("w_in", [C, RIN])
        w_ih = st.sb("w_ih", [128, KI, RH])
        xg_all = st.sb("xg_all", [128, 2, T, KH, B])
        w_hh = xg_all[:].rearrange("p a t k b -> p (a t k b)").rearrange("p (k m) -> p k m", k=KH)
        b_in = st.sb("b_in", [128, KI])
        b_ih = st.sb("b_ih", [128, KH])
        b_hh = st.sb("b_hh", [128, KH])
        b_g = st.sb("b_g", [128, KH])
        b_out = st.sb("b_out", [C, 1])
        stat_w = st.sb("stat_w", [C, 2, 32])
        ws = st.sb("ws", [C, 1])
        bs = st.sb("bs", [B, 1])
        mean_w = st.sb("mean_w", [C, C])
        w_abs = st.sb("w_abs", [128, 4, 2])
        w_scale = st.sb("w_scale", [128, 2, 2])
        w_hi = st.sb("w_hi", [128, KH, RH], F16)
        w_lo = st.sb("w_lo", [128, KH, RH], F16)
        w_hi_s = st.sb("w_hi_s", [128, KH, RH], F16)
        o_hi = st.sb("o_hi", [128, KH, C], F16)
        o_lo = st.sb("o_lo", [128, KH, C], F16)
        o_hi_s = st.sb("o_hi_s", [128, KH, C], F16)
        ws_c = st.sb("ws_c", [C, 1])
        h_hi = [st.sb(f"h_hi{p}", [128, KH, T, B], F16) for p in range(2)]
        h_lo = [st.sb(f"h_lo{p}", [128, KH, T, B], F16) for p in range(2)]
        h = [st.sb(f"h_{s}", [128, 2, B]) for s in "ab"]
        hi4 = [st.sb(f"hi4_{s}", [128, 2, B], F16) for s in "ab"]
        xg = [xg_all[:, p] for p in range(2)]
        pre = [[st.sb(f"pre{s}{i}", [128, 2, B]) for i in range(2)] for s in "ab"]
        xn = st.sb("xn", [C, T, B])
        xn_s = st.sb("xn_s", [C, T, B])
        tz = st.sb("tz", [128, KI, T * B])
        w_out = tz[:].rearrange("p k n -> p (k n)").rearrange("p (k m) -> p k m", k=KH)
        inp = st.sb("inp", [128, KI, T * B])
        yb = st.sb("yb", [C, T, B])
        y = st.sb("y", [C, T, B])
        ysq = st.sb("ysq", [C, T, B])
        rows = st.sb("rows", [96, B, T])
        sm = st.sb("sm", [B, 3, T])
        ln_t = st.sb("ln_t", [B, 5, T])
        one8 = st.sb("one8", [B, T])
        cur = [st.sb(f"cur{p}", [B, T]) for p in range(2)]
        half_neg = st.sb("half_neg2", [B, T])
        mem = st.sb("mem", [B, 1])
        memp = st.sb("memp", [B, T])

        ps_h = [[st.ps(f"ps_h{s}{i}", [128, 512]) for i in range(2)] for s in "ab"]
        ps_xg = [st.ps(f"ps_xg{i}", [128, 2, T * B]) for i in range(2)]
        ps_z = st.ps("ps_z", [128, KI, T * B])
        ps_y = st.ps("ps_y", [128, 512])

        loaded = st.sem("rnn_loaded")
        setup = st.sem("rnn_setup")
        mean_ready = st.sem("mean_ready")
        psum_ready = [st.sem(f"psum_ready_{s}") for s in "ab"]
        pre_ready = [st.sem(f"pre_ready_{s}") for s in "ab"]
        hi_ready = [st.sem(f"hi_ready_{s}") for s in "ab"]
        h_ready = [st.sem(f"h_ready_{s}") for s in "ab"]
        hi4_ready = [st.sem(f"hi4_ready_{s}") for s in "ab"]
        lo_ready = [st.sem(f"lo_ready_{s}") for s in "ab"]
        w_step = st.sem("w_step")
        w_max = st.sem("w_max")
        rows_ready = st.sem("rows_ready")
        rows_moved = st.sem("rows_moved")
        xn_step = st.sem("xn_step")
        xn_ready = st.sem("xn_ready")
        z_ready = st.sem("z_ready")
        tz_ready = st.sem("tz_ready")
        inp_ready = st.sem("inp_ready")
        xgp_ready = st.sem("xgp_ready")
        xg_ready = st.sem("xg_ready")
        yp_ready = st.sem("yp_ready")
        yb_ready = st.sem("yb_ready")
        y_ready = st.sem("y_ready")
        ysq_ready = st.sem("ysq_ready")
        y_stored = st.sem("y_stored")
        stp_ready = st.sem("stp_ready")
        var_ready = st.sem("var_ready")
        sm_ready = st.sem("sm_ready")
        ln_step = st.sem("ln_step")
        cur_ready = st.sem("cur_ready")
        memp_ready = st.sem("memp_ready")
        mem_ready = st.sem("mem_ready")

        NLOADS = 11
        SETUP = 11

        def tokens(g):
            return x_sb[:, :, bass.ds(g * T, T)].rearrange("c b l -> c l b")

        with nc.Block() as block:
            @block.sync
            def _(sp):
                for dst, name in ((w_in, "L0_conv_w_in"), (w_ih, "L0_conv_w_ih"),
                                  (b_in, "L0_conv_b_in"), (b_ih, "L0_conv_b_ih"),
                                  (b_hh, "L0_conv_b_hh"), (b_out, "L0_conv_b_out"), (ws, "L1_attn_Ws"),
                                  (mean_w, "c_mean")):
                    sp.dma_start(dst[:], d[name]).then_inc(loaded, 16)
                sp.dma_start(w_hh, d["L0_conv_w_hh"]).then_inc(loaded, 16)
                sp.dma_start(w_out, d["L0_conv_w_out"]).then_inc(loaded, 16)
                sp.dma_start(bs[:], d["L1_attn_bs"].partition_broadcast(B)).then_inc(loaded, 16)

                def move(g):
                    sp.wait_ge(rows_ready, g + 1)
                    if not isinstance(g, int) or g > 0:
                        sp.wait_ge(cur_ready, g)
                    for i in range(3):
                        sp.dma_start(sm[:, i, :], rows[32 * i:32 * i + 1, :, :]
                                     ).then_inc(rows_moved, 16)

                move(0)
                with sp.Fori(1, NBLK) as g:
                    move(g)
                sp.wait_ge(rows_moved, 48 * NBLK)

            def pe_inproj(pe, g):
                pe.wait_ge(xn_ready, g + 1)
                if not isinstance(g, int) or g > 0:
                    pe.wait_ge(inp_ready, g)
                for m in range(KI):
                    last = nc.tensor.matmul(ps_z[:, m, :], w_in[:, m * 128:(m + 1) * 128],
                                            xn[:].rearrange("c t b -> c (t b)"), start=(m == 0), stop=True,
                                            skip_group_check=True)
                last.then_inc(z_ready, 1)

            def pe_xgate(pe, g, m):
                if m == 0:
                    pe.wait_ge(inp_ready, g + 1)
                if m % 2 == 0 and (not isinstance(g, int) or g > 0):
                    pe.wait_ge(xg_ready, 2 * g - 1 + m // 2)
                for k in range(KI):
                    last = nc.tensor.matmul(ps_xg[m // 2][:, m % 2, :], w_ih[:, k, m * 128:(m + 1) * 128],
                                            inp[:, k, :], start=(m % 2 == 0 and k == 0), stop=(k == KI - 1),
                                            skip_group_check=True)
                if m % 2 == 1:
                    last.then_inc(xgp_ready, 1)

            def pe_yproj(pe, g, p, half):
                if half == 0 and after(g):
                    pe.wait_ge(rows_ready, g)
                for k in (2 * half, 2 * half + 1):
                    for n, (w, hx) in enumerate(((o_hi, h_hi), (o_lo, h_hi), (o_hi_s, h_lo))):
                        last = nc.tensor.matmul(ps_y[:, 0:T * B], w[:, k, :],
                                                hx[p][:, k].rearrange("q t b -> q (t b)"),
                                                start=(k == 0 and n == 0), stop=(k == KH - 1 and n == 2),
                                                skip_group_check=True)
                if half == 1:
                    last.then_inc(yp_ready, 1)

            def pe_stats(pe, g):
                pe.wait_ge(y_ready, g + 1)
                for i in range(2):
                    nc.tensor.matmul(ps_y[32 * i:32 * i + 32, 0:T * B], stat_w[:, i, :],
                                     y[:].rearrange("c t b -> c (t b)"), start=True, stop=True)
                pe.wait_ge(ysq_ready, g + 1)
                nc.tensor.matmul(ps_y[64:96, 0:T * B], stat_w[:, 0, :], ysq[:].rearrange("c t b -> c (t b)"),
                                 start=True, stop=True).then_inc(stp_ready, 1)

            def pe_block(pe, g, p, ahead1=True, ahead2=True, behind=True):
                for s in range(T):
                    i = s % 2
                    q, r = (p, s - 1) if s else (1 - p, T - 1)

                    def mm(half, ks, w, hx, first=False, last=False):
                        for k in ks:
                            for m in (2 * half, 2 * half + 1):
                                ins = nc.tensor.matmul(ps_h[half][i][:, (m % 2) * B:(m % 2 + 1) * B],
                                                       w[:, k, m * 128:(m + 1) * 128], hx[q][:, k, r, :],
                                                       start=(first and k == 0 and m % 2 == 0), stop=last,
                                                       skip_group_check=True)
                        if last:
                            ins.then_inc(psum_ready[half], 1)

                    lo_chunks, hi_chunks = (0, 1), (2, 3)
                    pe.wait_ge(hi_ready[0], g * T + s + 1)
                    for half in range(2):
                        mm(half, lo_chunks, w_hi, h_hi, first=True)
                        mm(half, lo_chunks, w_lo, h_hi)
                    pe.wait_ge(hi_ready[1], g * T + s + 1)
                    mm(0, hi_chunks, w_hi, h_hi)
                    mm(0, hi_chunks, w_lo, h_hi)
                    pe.wait_ge(lo_ready[0], g * T + s + 1)
                    mm(0, lo_chunks, w_hi_s, h_lo)
                    mm(1, lo_chunks, w_hi_s, h_lo)
                    pe.wait_ge(lo_ready[1], g * T + s + 1)
                    mm(0, hi_chunks, w_hi_s, h_lo, last=True)
                    mm(1, hi_chunks, w_hi, h_hi)
                    mm(1, hi_chunks, w_lo, h_hi)
                    mm(1, hi_chunks, w_hi_s, h_lo, last=True)
                    if s in (0, 1) and behind:
                        pe_yproj(pe, g - 1, 1 - p, s)
                    if s in (2, 3, 5, 6) and ahead1:
                        pe_xgate(pe, g + 1, (2, 3, 5, 6).index(s))
                    if s == 4 and behind:
                        pe_stats(pe, g - 1)
                    if s == 7 and ahead2:
                        pe_inproj(pe, g + 2)

            def act_z(act, g):
                act.wait_ge(z_ready, g + 1)
                if not isinstance(g, int) or g > 0:
                    act.wait_ge(inp_ready, g)
                for m in range(KI):
                    last = nc.scalar.activation(tz[:, m, :], ps_z[:, m, :], ACT.Tanh, bias=b_in[:, m:m + 1])
                last.then_inc(tz_ready, 1)

            def act_xg(act, g, p, half):
                act.wait_ge(xgp_ready, 2 * g + half + 1)
                for m in (2 * half, 2 * half + 1):
                    last = nc.scalar.activation(xg[p][:, :, m, :],
                                                ps_xg[half][:, m % 2, :].rearrange("q (t b) -> q t b", b=B),
                                                ACT_ID, bias=b_g[:, m:m + 1])
                last.then_inc(xg_ready, 1)

            def act_rows(act, g):
                act.wait_ge(stp_ready, g + 1)
                if not isinstance(g, int) or g > 0:
                    act.wait_ge(rows_moved, 48 * g)
                nc.scalar.copy(rows[:].rearrange("q b t -> q t b"),
                               ps_y[0:96, 0:T * B].rearrange("q (t b) -> q t b", b=B)).then_inc(rows_ready, 1)

            def act_y(act, g):
                act.wait_ge(yp_ready, g + 1)
                if after(g):
                    act.wait_ge(y_ready, g)
                nc.scalar.activation(yb[:], ps_y[:, 0:T * B].rearrange("c (t b) -> c t b", b=B), ACT_ID,
                                     bias=b_out[:, 0:1], scale=w_scale[:, 1, 1:2]).then_inc(yb_ready, 1)

            def act_block(act, g, p, ahead1=True, ahead2=True, behind=True):
                for s in range(T):
                    for half in range(2):
                        act.wait_ge(pre_ready[half], g * T + s + 1)
                        nc.scalar.activation(h_hi[p][:, 2 * half:2 * half + 2, s, :], pre[half][s % 2][:],
                                             ACT.Tanh).then_inc(hi_ready[half], 1)
                        nc.scalar.activation(h[half][:], pre[half][s % 2][:], ACT.Tanh).then_inc(h_ready[half], 1)
                    if s == 1 and behind:
                        act_y(act, g - 1)
                    if s == 3 and ahead1:
                        act_xg(act, g + 1, 1 - p, 0)
                    if s == 4 and behind:
                        act_rows(act, g - 1)
                    if s == 6 and ahead1:
                        act_xg(act, g + 1, 1 - p, 1)
                    if s == 7 and ahead2:
                        act_z(act, g + 2)

            def dve_inp(dve, g, m):
                if m == 0:
                    dve.wait_ge(tz_ready, g + 1)
                    if after(g):
                        dve.wait_ge(xgp_ready, 2 * g)
                ins = nc.vector.scalar_tensor_tensor(inp[:, m, :], ps_z[:, m, :], b_in[:, m:m + 1], tz[:, m, :],
                                                     ALU.add, ALU.subtract)
                if m == KI - 1:
                    ins.then_inc(inp_ready, 1)

            def dve_guard(dve, g):
                dve.wait_ge(var_ready, g + 1)
                nc.vector.tensor_scalar(ln_t[:, 2, :], ln_t[:, 1, :], 0.0, 1e-5, ALU.max, ALU.add
                                        ).then_inc(sm_ready, 1)

            def dve_decay(dve, g, p, s):
                if s == 0:
                    dve.wait_ge(cur_ready, g + 1)
                if s or after(g):
                    dve.wait_ge(mem_ready, g * (T + 1) + s)
                nc.vector.scalar_tensor_tensor(memp[:, s:s + 1], mem[:], DECAY, cur[p][:, s:s + 1], ALU.mult, ALU.add
                                               ).then_inc(memp_ready, 1)

            def dve_reset(dve, g, s):
                dve.wait_ge(memp_ready, g * T + s + 1)
                nc.vector.scalar_tensor_tensor(mem[:], memp[:, s:s + 1], 1.0, memp[:, s:s + 1],
                                               ALU.is_lt, ALU.mult).then_inc(mem_ready, 1)
                if s == T - 1:
                    nc.vector.tensor_scalar(spikes[:, bass.ds(g * T, T)], memp[:], 1.0, None, ALU.is_ge
                                            ).then_inc(mem_ready, 1)

            def dve_block(dve, g, p, ahead1=True, behind=True, behind2=True):
                dve.wait_ge(xg_ready, 2 * g + 2)
                for s in range(T):
                    for half in range(2):
                        dve.wait_ge(psum_ready[half], g * T + s + 1)
                        nc.vector.scalar_tensor_tensor(
                            pre[half][s % 2][:].rearrange("q m b -> q (m b)"), ps_h[half][s % 2][:, 0:2 * B],
                            w_scale[:, 1, 0:1], xg[p][:, s, 2 * half:2 * half + 2, :].rearrange("q m b -> q (m b)"),
                            ALU.mult, ALU.add).then_inc(pre_ready[half], 1)
                    dve.wait_ge(hi_ready[1], g * T + s + 2)
                    for half in range(2):
                        if half == 1:
                            dve.wait_ge(h_ready[1], g * T + s + 1)
                        nc.vector.tensor_scalar(hi4[half][:], h_hi[p][:, 2 * half:2 * half + 2, s, :], LO_SCALE, None,
                                                ALU.mult).then_inc(hi4_ready[half], 1)
                    for half in range(2):
                        dve.wait_ge(hi4_ready[half], g * T + s + 1)
                        nc.vector.scalar_tensor_tensor(h_lo[p][:, 2 * half:2 * half + 2, s, :], h[half][:], LO_SCALE,
                                                       hi4[half][:], ALU.mult, ALU.subtract
                                                       ).then_inc(lo_ready[half], 1)
                    if behind2:
                        dve_decay(dve, g - 2, p, s)
                    if s in (0, 1) and ahead1:
                        dve_inp(dve, g + 1, s)
                    if s == T - 1 and behind:
                        dve_guard(dve, g - 1)
                    if behind2:
                        dve_reset(dve, g - 2, s)

            def pool_xn(pool, g):
                if not isinstance(g, int) or g > 0:
                    pool.wait_ge(z_ready, g)
                nc.gpsimd.tensor_tensor(xn_s[:], tokens(g), scale_cb[:].unsqueeze(1).to_broadcast([C, T, B]),
                                        ALU.mult).then_inc(xn_step, 1)
                pool.wait_ge(xn_step, g + 1)
                nc.gpsimd.tensor_tensor(xn[:], xn_s[:], shift_cb[:].unsqueeze(1).to_broadcast([C, T, B]),
                                        ALU.add).then_inc(xn_ready, 1)

            def pool_y(pool, g):
                pool.wait_ge(yb_ready, g + 1)
                if after(g):
                    pool.wait_ge(stp_ready, g)
                nc.gpsimd.tensor_tensor(y[:], yb[:], tokens(g), ALU.add).then_inc(y_ready, 1)
                pool.wait_ge(y_ready, g + 1)
                nc.gpsimd.tensor_tensor(ysq[:], y[:], y[:], ALU.mult).then_inc(ysq_ready, 1)
                nc.gpsimd.tensor_copy(tokens(g), y[:]).then_inc(y_stored, 1)

            def pool_ln(pool, g, p, free=True):
                pool.wait_ge(rows_moved, 48 * g + 48)
                mean, dot, square = sm[:, 0, :], sm[:, 1, :], sm[:, 2, :]
                r = ln_t[:, 3, :]
                ch = Chain(pool, ln_step, g * 3)
                ch.step(nc.gpsimd.tensor_tensor(ln_t[:, 0, :], mean, mean, ALU.mult))
                nc.gpsimd.tensor_tensor(ln_t[:, 1, :], square, ln_t[:, 0, :], ALU.subtract).then_inc(var_ready, 1)
                pool.wait_ge(sm_ready, g + 1)
                ch.step(nc.gpsimd.tensor_tensor(r, ln_t[:, 2, :], half_neg[:], ALU.pow))
                nc.gpsimd.tensor_tensor(ln_r[:, bass.ds(g * T, T)], r, one8[:], ALU.mult)
                nc.gpsimd.tensor_tensor(ln_mr[:, bass.ds(g * T, T)], mean, r, ALU.mult)
                ch.step(nc.gpsimd.tensor_tensor(ln_t[:, 4, :], dot, r, ALU.mult))
                if free:
                    pool.wait_ge(mem_ready, (g - 1) * (T + 1))
                nc.gpsimd.tensor_tensor(cur[p][:], ln_t[:, 4, :], bs[:, 0:1].to_broadcast([B, T]), ALU.add
                                        ).then_inc(cur_ready, 1)

            def pool_block(pool, g, p, ahead2=True, behind=True, behind2=True):
                if ahead2:
                    pool_xn(pool, g + 2)
                if behind:
                    pool_y(pool, g - 1)
                    pool_ln(pool, g - 1, 1 - p, behind2)

            FRONT, TAIL = 4, 2

            def run(eng, one):
                for g in range(FRONT):
                    one(eng, g, g % 2)
                with eng.Fori(0, (NBLK - FRONT - TAIL) // 2) as it:
                    for q in range(2):
                        one(eng, it * 2 + (FRONT + q), q)
                for g in range(NBLK - TAIL, NBLK):
                    one(eng, g, g % 2)

            def near(g, lo=0, hi=NBLK):
                return not isinstance(g, int) or lo <= g < hi

            @block.tensor
            def _(pe):
                pe.wait_ge(loaded, 16 * NLOADS)
                nc.tensor.matmul(ps_y[:, 0:1], mean_w[:], ws[:]).then_inc(mean_ready, 1)
                pe.wait_ge(setup, SETUP)
                pe_inproj(pe, 0)
                for m in range(KH):
                    pe_xgate(pe, 0, m)
                pe_inproj(pe, 1)
                run(pe, lambda e, g, p: pe_block(e, g, p, near(g + 1), near(g + 2), near(g - 1)))
                for half in range(2):
                    pe.wait_ge(lo_ready[half], L + 1)
                pe_yproj(pe, NBLK - 1, 1, 0)
                pe_yproj(pe, NBLK - 1, 1, 1)
                pe_stats(pe, NBLK - 1)

            @block.scalar
            def _(act):
                act.wait_ge(loaded, 16 * NLOADS)
                act.wait_ge(setup, SETUP)
                act_z(act, 0)
                act_xg(act, 0, 0, 0)
                act_xg(act, 0, 0, 1)
                act_z(act, 1)
                run(act, lambda e, g, p: act_block(e, g, p, near(g + 1), near(g + 2), near(g - 1)))
                act_y(act, NBLK - 1)
                act_rows(act, NBLK - 1)

            @block.vector
            def _(dve):
                v = nc.vector
                dve.wait_ge(loaded, 16 * NLOADS)
                v.tensor_reduce(w_abs[:, 0, 0:1], w_hh.rearrange("p k m -> p (k m)"), AX_X, ALU.max,
                                apply_absolute_value=True)
                v.tensor_reduce(w_abs[:, 0, 1:2], w_out.rearrange("p k m -> p (k m)"), AX_X, ALU.max,
                                apply_absolute_value=True).then_inc(w_max, 1)
                v.memset(mem[:], 0.0).then_inc(setup, 1)
                v.memset(half_neg[:], -0.5).then_inc(setup, 1)
                v.memset(one8[:], 1.0).then_inc(setup, 1)
                v.tensor_tensor(b_g[:], b_ih[:], b_hh[:], ALU.add).then_inc(setup, 1)
                for half in range(2):
                    ks = slice(2 * half, 2 * half + 2)
                    v.memset(h_hi[1][:, ks, T - 1, :], 0.0).then_inc(hi_ready[half], 1)
                    v.memset(h_lo[1][:, ks, T - 1, :], 0.0).then_inc(lo_ready[half], 1)
                dve.wait_ge(w_max, 2)
                ch = Chain(dve, w_step)
                ch.step(v.tensor_scalar(w_abs[:, 3, :], w_abs[:, 1, :], 1e-30, None, ALU.max))
                ch.step(v.tensor_scalar(w_abs[:, 2, :].bitcast(I32), w_abs[:, 3, :].bitcast(I32), 0x7F800000, None,
                                        ALU.bitwise_and))
                ch.step(v.reciprocal(w_abs[:, 3, :], w_abs[:, 2, :]))
                ch.step(v.tensor_scalar(w_scale[:, 0, :], w_abs[:, 3, :], W_TOP, None, ALU.mult))
                v.tensor_scalar(w_scale[:, 1, :], w_abs[:, 2, :], 1.0 / W_TOP, None, ALU.mult).then_inc(setup, 1)
                for i, (w, hi, lo, hi_s) in enumerate(((w_hh, w_hi, w_lo, w_hi_s), (w_out, o_hi, o_lo, o_hi_s))):
                    scale = w_scale[:, 0, i:i + 1]
                    ch.step(v.tensor_scalar(hi[:], w, scale, None, ALU.mult))
                    v.scalar_tensor_tensor(lo[:], w, scale, hi[:], ALU.mult, ALU.subtract).then_inc(setup, 1)
                    v.tensor_scalar(hi_s[:], hi[:], 1.0 / LO_SCALE, None, ALU.mult).then_inc(setup, 1)
                dve.wait_ge(mean_ready, 1)
                ch.step(v.tensor_tensor(ws_c[:], ws[:], ps_y[:, 0:1], ALU.subtract))
                v.memset(stat_w[:, 0, :], 1.0 / C).then_inc(setup, 1)
                v.tensor_copy(stat_w[:, 1, :], ws_c[:].to_broadcast([C, 32])).then_inc(setup, 1)
                dve.wait_ge(setup, SETUP)
                dve_inp(dve, 0, 0)
                dve_inp(dve, 0, 1)
                run(dve, lambda e, g, p: dve_block(e, g, p, near(g + 1), near(g - 1), near(g - 2)))
                dve_guard(dve, NBLK - 1)
                for g in (NBLK - 2, NBLK - 1):
                    for s in range(T):
                        dve_decay(dve, g, g % 2, s)
                        dve_reset(dve, g, s)

            @block.gpsimd
            def _(pool):
                pool.wait_ge(w_max, 1)
                nc.gpsimd.partition_all_reduce(w_abs[:, 1, :], w_abs[:, 0, :], 128, bass.bass_isa.ReduceOp.max
                                               ).then_inc(w_max, 1)
                pool.wait_ge(setup, SETUP)
                pool.wait_ge(loaded, 16 * NLOADS)
                pool_xn(pool, 0)
                pool_xn(pool, 1)
                run(pool, lambda e, g, p: pool_block(e, g, p, near(g + 2), near(g - 1), near(g - 2)))
                pool_y(pool, NBLK - 1)
                pool_ln(pool, NBLK - 1, 1)


def after(g, n=1):
    return not isinstance(g, int) or g >= n


def apart(eng, sem):
    eng.sem_inc(sem, 1)


def pipelined(eng, count, front, tail, one):
    for i in range(front):
        one(i, i // 2, i % 2)
    with eng.Fori(0, (count - front - tail) // 2) as it:
        for p in range(2):
            one(it * 2 + (front + p), it + front // 2, p)
    for i in range(count - tail, count):
        one(i, i // 2, i % 2)


def build_mask(nc, d, spikes, ln_r, ln_mr, mask, wvo, bvo):
    with ExitStack() as ctx:
        st = Store(nc, ctx)
        ones = st.sb("ones", [B, Q])
        key_bias = st.sb("key_bias", [Q, L])
        local_bias = st.sb("local_bias", [Q, L])
        tri = st.sb("tri", [Q, 2 * Q])
        wv_t = st.sb("wv_t", [C, C])
        wo = st.sb("wo", [C, C])
        bv = st.sb("bv", [C, 1])
        bv_cols = st.sb("bv_cols", [C, C])
        ps_n = st.ps("ps_n", [Q, 2, 512])
        ps_w = st.ps("ps_w", [C, 2, 512])
        loaded = st.sem("mask_loaded")
        ready = st.sem("mask_inputs_ready")
        counted = st.sem("counted")
        step = st.sem("mask_step")
        saved = st.sem("ln_saved")

        with nc.Block() as block:
            @block.sync
            def _(sp):
                for dst, name in ((tri, "c_tri"), (wv_t, "L1_attn_Wv"), (wo, "L1_attn_Wo"), (bv, "L1_attn_bv")):
                    sp.dma_start(dst[:], d[name]).then_inc(loaded, 16)
                sp.dma_start(d["s_ln"][0], ln_r[:]).then_inc(saved, 16)
                sp.dma_start(d["s_ln"][1], ln_mr[:]).then_inc(saved, 16)
                sp.wait_ge(saved, 32)

            @block.tensor
            def _(pe):
                pe.wait_ge(ready, 1)
                for h in range(2):
                    last = nc.tensor.matmul(ps_n[:, h, :], ones[:], spikes[:, h * 512:(h + 1) * 512])
                last.then_inc(counted, 1)
                pe.wait_ge(loaded, 64)
                nc.tensor.matmul(ps_w[:, 0, 0:C], wv_t[:], wo[:])
                pe.wait_ge(ready, 2)
                nc.tensor.matmul(ps_w[:, 1, 0:C], bv_cols[:], wo[:]).then_inc(counted, 1)

            @block.vector
            def _(dve):
                v = nc.vector
                v.memset(ones[:], 1.0).then_inc(ready, 1)
                dve.wait_ge(loaded, 64)
                v.tensor_copy(bv_cols[:], bv[:, 0:1].to_broadcast([C, C])).then_inc(ready, 1)
                dve.wait_ge(counted, 1)
                ch = Chain(dve, step)
                ch.step(v.tensor_scalar(key_bias[:], ps_n[:].rearrange("p a b -> p (a b)"), 0.5, NEG,
                                        ALU.is_lt, ALU.mult))
                ch.step(v.tensor_copy(local_bias[:], key_bias[:]))
                ch.step(v.memset(local_bias[:].rearrange("p (a b) -> p a b", b=STRIDE)[:, :, 0], NEG))
                ch.step(v.memset(local_bias[:, 0:FIRST], NEG))
                for i in range(NQ):
                    lo = 0 if i else Q
                    v.tensor_tensor(mask[:, i, lo:2 * Q], tri[:, lo:2 * Q],
                                    local_bias[:, (i - 1) * Q + lo:(i + 1) * Q], ALU.add)
                    v.tensor_copy(mask[:, i, 2 * Q:2 * Q + FIRST], key_bias[:, 0:FIRST])
                    v.tensor_copy(mask[:, i, 2 * Q + FIRST:],
                                  key_bias[:].rearrange("p (a b) -> p a b", b=STRIDE)[:, 1:, 0])
                dve.wait_ge(counted, 2)
                v.tensor_copy(wvo[:], ps_w[:, 0, 0:C])
                v.tensor_copy(bvo[:], ps_w[:, 1, 0:C])


def attention(nc, d, x_sb, mask, wvo, bvo):
    NK = 2 * Q + NG
    LAG_T, LAG_V = 2, 3
    with ExitStack() as ctx:
        st = Store(nc, ctx)
        wq, wk = st.sb("wq", [C, C]), st.sb("wk", [C, C])
        bq, bk, bo = st.sb("bq", [C, 1]), st.sb("bk", [C, 1]), st.sb("bo", [C, 1])
        ident = st.sb("ident", [128, 128])
        r_b, mr_b = st.sb("r_b", [C, L]), st.sb("mr_b", [C, L])
        xr = st.sb("xr", [C, L])
        ln = st.sb("ln", [C, L])
        ln_g = st.sb("ln_g", [C, NG])
        qt = [st.sb(f"qt{p}", [C, L]) for p in range(2)]
        kt = [st.sb(f"kt{p}", [C, NQ, NK]) for p in range(2)]
        vt = [st.sb(f"vt{p}", [Q, NQ, C]) for p in range(2)]
        vg = [st.sb(f"vg{p}", [NG, C]) for p in range(2)]
        pr = [st.sb(f"pr{i}", [Q, NK]) for i in range(4)]
        pt = [st.sb(f"pt{i}", [Q, 3, Q]) for i in range(2)]
        mx, nm, den, rden, rv = (st.sb(n, [Q, 2 * NQ]) for n in ("mx", "nm", "den", "rden", "rv"))
        ps_p = [st.ps(f"ps_p{i}", [128, 512]) for i in range(2)]
        ps_s = [st.ps(f"ps_s{i}", [128, 512]) for i in range(2)]
        ps_t = [st.ps(f"ps_t{i}", [128, 4, Q]) for i in range(2)]
        ps_o = [st.ps(f"ps_o{i}", [128, 512]) for i in range(2)]

        loaded = st.sem("attn_loaded")
        waits_apart = st.sem("attn_waits_apart")
        bc_loaded = st.sem("ln_factors_loaded")
        xr_ready = st.sem("xr_ready")
        ln_ready = st.sem("ln_ready")
        lng_ready = st.sem("lng_ready")
        proj_done = st.sem("proj_done")
        qk_evac = st.sem("qk_evac")
        v_evac = st.sem("v_evac")
        kt_ready = st.sem("kt_ready")
        s_done = st.sem("s_done")
        masked = st.sem("masked")
        nm_ready = st.sem("nm_ready")
        exp_done = st.sem("exp_done")
        norm_step = st.sem("norm_step")
        p_ready = st.sem("p_ready")
        t_done = st.sem("t_done")
        pt_ready = st.sem("pt_ready")
        pv_done = st.sem("pv_done")
        o_added = st.sem("o_added")

        def back(b, p, i, lag):
            return (b, p, i - lag) if i >= lag else (b - 1, 1 - p, i - lag + NQ)

        def xb(b):
            return x_sb[:, bass.ds(b, 1), :].rearrange("c b l -> c (b l)")

        with nc.Block() as block:
            @block.sync
            def _(sp):
                for dst, name in ((wq, "L1_attn_Wq"), (wk, "L1_attn_Wk"), (bq, "L1_attn_bq"), (bk, "L1_attn_bk"),
                                  (bo, "L1_attn_bo"), (ident, "c_ident")):
                    sp.dma_start(dst[:], d[name]).then_inc(loaded, 16)

                def factors(b):
                    if after(b):
                        sp.wait_ge(ln_ready, b)
                    for i, dst in enumerate((r_b, mr_b)):
                        sp.dma_start(dst[:], d["s_ln"][i, bass.ds(b, 1), :].rearrange("b l -> (b l)")
                                     .partition_broadcast(C)).then_inc(bc_loaded, 16)

                factors(0)
                with sp.Fori(1, B) as b:
                    factors(b)
                sp.wait_ge(bc_loaded, 32 * B)

            def pe_proj(pe, b, p, piece):
                kind, h = ("q", 0), ("q", 1)
                kind, h = (("q", 0), ("q", 1), ("k", 0), ("k", 1), ("v", 0), ("v", 1), ("g", 0))[piece]
                bank = ps_p[h]
                if piece == 0:
                    pe.wait_ge(ln_ready, b + 1)
                    if after(b):
                        pe.wait_ge(v_evac, 3 * b)
                if piece in (2, 3, 4, 5):
                    pe.wait_ge(qk_evac, 4 * b + piece - 1)
                if kind in "qk":
                    last = nc.tensor.matmul(bank[:], (wq if kind == "q" else wk)[:], ln[:, h * 512:(h + 1) * 512])
                elif kind == "v":
                    for i in range(4):
                        j = 4 * h + i
                        last = nc.tensor.matmul(bank[:, i * C:(i + 1) * C], ln[:, j * Q:(j + 1) * Q], wvo[:],
                                                start=(i == 0), stop=True, skip_group_check=True)
                else:
                    pe.wait_ge(lng_ready, b + 1)
                    pe.wait_ge(v_evac, 3 * b + 1)
                    last = nc.tensor.matmul(bank[0:NG, 0:C], ln_g[:], wvo[:])
                last.then_inc(proj_done, 1)

            def pe_scores(pe, b, p, i):
                n = b * NQ + i
                if i == 0:
                    pe.wait_ge(kt_ready, b + 1)
                if after(n, 2):
                    pe.wait_ge(masked, n - 1)
                lo = 0 if i else Q
                nc.tensor.matmul(ps_s[i % 2][:, lo:NK], qt[p][:, i * Q:(i + 1) * Q], kt[p][:, i, lo:NK]
                                 ).then_inc(s_done, 1)

            def pe_transpose(pe, b, p, i):
                n = b * NQ + i
                pe.wait_ge(p_ready, n + 1)
                if after(n, 2):
                    pe.wait_ge(pt_ready, n - 1)
                w = pr[i % 4]
                out = ps_t[i % 2]
                if i:
                    nc.tensor.transpose(out[:, 0, :], w[:, 0:Q], ident[:])
                nc.tensor.transpose(out[:, 1, :], w[:, Q:2 * Q], ident[:])
                nc.tensor.transpose(out[0:NG, 2, :], w[:, 2 * Q:NK], ident[:]).then_inc(t_done, 1)

            def pe_values(pe, b, p, i):
                n = b * NQ + i
                pe.wait_ge(pt_ready, n + 1)
                if i == 0:
                    pe.wait_ge(v_evac, 3 * b + 3)
                if i % 4 == 0 and after(b):
                    pe.wait_ge(o_added, 2 * b + i // 4 - 1)
                out = ps_o[i // 4][:, (i % 4) * Q:(i % 4 + 1) * Q]
                w = pt[i % 2]
                if i:
                    nc.tensor.matmul(out, vt[p][:, i - 1, :], w[:, 0, :], start=(i % 4 == 0), stop=False,
                                     skip_group_check=True)
                nc.tensor.matmul(out, vt[p][:, i, :], w[:, 1, :], start=(i == 0), stop=False, skip_group_check=True)
                nc.tensor.matmul(out, vg[p][:], w[0:NG, 2, :], start=False, stop=True, skip_group_check=True
                                 ).then_inc(pv_done, 1)

            @block.tensor
            def _(pe):
                pe.wait_ge(loaded, 96)
                for piece in range(7):
                    pe_proj(pe, 0, 0, piece)

                def one(b, half, p):
                    for i in range(NQ):
                        pe_scores(pe, b, p, i)
                        if i >= LAG_T or after(b):
                            pe_transpose(pe, *back(b, p, i, LAG_T))
                        if i >= LAG_V or after(b):
                            pe_values(pe, *back(b, p, i, LAG_V))
                        if i >= 2 and not (isinstance(b, int) and b == B - 1):
                            pe_proj(pe, b + 1, 1 - p, i - 2)
                            if i == NQ - 1:
                                pe_proj(pe, b + 1, 1 - p, 6)

                pipelined(pe, B, 2, 2, one)
                for i in range(LAG_V):
                    if i < LAG_T:
                        pe_transpose(pe, B - 1, 1, NQ - LAG_T + i)
                    pe_values(pe, B - 1, 1, NQ - LAG_V + i)

            def act_proj(act, b, p, piece):
                act.wait_ge(proj_done, 7 * b + piece + 1)
                h = piece % 2
                if piece < 2:
                    nc.scalar.activation(qt[p][:, h * 512:(h + 1) * 512], ps_p[h][:], ACT_ID, bias=bq[:, 0:1]
                                         ).then_inc(qk_evac, 1)
                else:
                    nc.scalar.activation(kt[p][:, 4 * h:4 * h + 4, Q:2 * Q],
                                         ps_p[h][:].rearrange("c (i q) -> c i q", q=Q), ACT_ID, bias=bk[:, 0:1]
                                         ).then_inc(qk_evac, 1)

            def act_exp(act, b, p, i):
                n = b * NQ + i
                lo, c = (0 if i else Q), NQ * p + i
                act.wait_ge(nm_ready, n + 1)
                nc.scalar.activation(pr[i % 4][:, lo:NK], pr[i % 4][:, lo:NK], ACT.Exp, bias=nm[:, c:c + 1],
                                     scale=SCALE, accum_out=den[:, c:c + 1]).then_inc(exp_done, 1)

            def act_pt(act, b, p, i):
                n = b * NQ + i
                act.wait_ge(t_done, n + 1)
                if after(n, 2):
                    act.wait_ge(pv_done, n - 1)
                lo = 0 if i else 1
                nc.scalar.copy(pt[i % 2][:, lo:2, :], ps_t[i % 2][:, lo:2, :])
                nc.scalar.copy(pt[i % 2][0:NG, 2, :], ps_t[i % 2][0:NG, 2, :]).then_inc(pt_ready, 1)

            @block.scalar
            def _(act):
                act.wait_ge(loaded, 96)
                for piece in range(4):
                    act_proj(act, 0, 0, piece)

                def one(b, half, p):
                    for i in range(NQ):
                        if i >= LAG_T or after(b):
                            act_pt(act, *back(b, p, i, LAG_T))
                        act_exp(act, b, p, i)
                        if 2 <= i < 6 and not (isinstance(b, int) and b == B - 1):
                            act_proj(act, b + 1, 1 - p, i - 2)

                pipelined(act, B, 2, 2, one)
                for i in range(NQ - LAG_T, NQ):
                    act_pt(act, B - 1, 1, i)

            def dve_ln(dve, b):
                dve.wait_ge(bc_loaded, 32 * b + 32)
                if after(b):
                    dve.wait_ge(ln_ready, b)
                nc.vector.tensor_tensor(xr[:], xb(b), r_b[:], ALU.mult).then_inc(xr_ready, 1)

            def dve_values(dve, b, p, piece):
                dve.wait_ge(proj_done, 7 * b + 5 + piece)
                if piece < 2:
                    nc.vector.tensor_tensor(vt[p][:, 4 * piece:4 * piece + 4, :],
                                            ps_p[piece][:].rearrange("q (i c) -> q i c", c=C),
                                            bvo[:].unsqueeze(1).to_broadcast([Q, 4, C]), ALU.add
                                            ).then_inc(v_evac, 1)
                else:
                    nc.vector.tensor_tensor(vg[p][:], ps_p[0][0:NG, 0:C], bvo[0:NG, :], ALU.add).then_inc(v_evac, 1)

            def dve_mask(dve, b, p, i):
                n = b * NQ + i
                lo, c = (0 if i else Q), NQ * p + i
                dve.wait_ge(s_done, n + 1)
                if after(n, 4):
                    dve.wait_ge(t_done, n - 3)
                apart(dve, waits_apart)
                nc.vector.tensor_tensor_reduce(pr[i % 4][:, lo:NK], ps_s[i % 2][:, lo:NK], mask[:, i, lo:NK], 1.0,
                                               -3.0e38, ALU.add, ALU.max, mx[:, c:c + 1]).then_inc(masked, 1)
                dve.wait_ge(masked, n + 1)
                nc.vector.tensor_scalar(nm[:, c:c + 1], mx[:, c:c + 1], -SCALE, None, ALU.mult).then_inc(nm_ready, 1)

            def dve_norm(dve, b, p, i):
                n = b * NQ + i
                lo, c = (0 if i else Q), NQ * p + i
                dve.wait_ge(exp_done, n + 1)
                ch = Chain(dve, norm_step, n * 2)
                ch.step(nc.vector.reciprocal(rden[:, c:c + 1], den[:, c:c + 1]))
                ch.step(nc.vector.scalar_tensor_tensor(rv[:, c:c + 1], mx[:, c:c + 1], NEG / 2, rden[:, c:c + 1],
                                                       ALU.is_gt, ALU.mult))
                nc.vector.tensor_scalar(pr[i % 4][:, lo:NK], pr[i % 4][:, lo:NK], rv[:, c:c + 1], None, ALU.mult
                                        ).then_inc(p_ready, 1)

            def dve_out(dve, b, h):
                dve.wait_ge(pv_done, b * NQ + 4 * h + 4)
                xs = xb(b)[:, h * 512:(h + 1) * 512]
                nc.vector.scalar_tensor_tensor(xs, ps_o[h][:], bo[:, 0:1], xs, ALU.add, ALU.add).then_inc(o_added, 1)

            @block.vector
            def _(dve):
                dve.wait_ge(loaded, 96)
                dve_ln(dve, 0)
                for piece in range(3):
                    dve_values(dve, 0, 0, piece)

                def one(b, half, p):
                    more = not (isinstance(b, int) and b == B - 1)
                    for i in range(NQ):
                        if i == 7 and more:
                            dve_values(dve, b + 1, 1 - p, 0)
                        dve_mask(dve, b, p, i)
                        if i == 0 and after(b):
                            for piece in (1, 2):
                                dve_values(dve, b, p, piece)
                        if i >= 1 or after(b):
                            dve_norm(dve, *back(b, p, i, 1))
                        if i == 0 and more:
                            dve_ln(dve, b + 1)
                        if i == 3 and after(b):
                            dve_out(dve, b - 1, 1)
                        if i == 7:
                            dve_out(dve, b, 0)

                pipelined(dve, B, 2, 2, one)
                dve_norm(dve, B - 1, 1, NQ - 1)
                dve_out(dve, B - 1, 1)

            @block.gpsimd
            def _(pool):
                def prepare(b, p):
                    pool.wait_ge(xr_ready, b + 1)
                    if after(b):
                        pool.wait_ge(proj_done, 7 * b)
                    nc.gpsimd.tensor_tensor(ln[:], xr[:], mr_b[:], ALU.subtract).then_inc(ln_ready, 1)
                    pool.wait_ge(ln_ready, b + 1)
                    apart(pool, waits_apart)
                    by_stride = ln[:].rearrange("c (a s) -> c a s", s=STRIDE)
                    nc.gpsimd.tensor_copy(ln_g[:, 0:FIRST], ln[:, 0:FIRST])
                    nc.gpsimd.tensor_copy(ln_g[:, FIRST:], by_stride[:, 1:, 0]).then_inc(lng_ready, 1)

                def keys(b, p):
                    pool.wait_ge(qk_evac, 4 * b + 4)
                    apart(pool, waits_apart)
                    k = kt[p]
                    nc.gpsimd.tensor_copy(k[:, 1:NQ, 0:Q], k[:, 0:NQ - 1, Q:2 * Q])
                    nc.gpsimd.tensor_copy(k[:, :, 2 * Q:2 * Q + FIRST],
                                          k[:, 0:1, Q:Q + FIRST].to_broadcast([C, NQ, FIRST]))
                    last = None
                    for j in range(1, L // STRIDE):
                        col = 2 * Q + FIRST + j - 1
                        src = k[:, j // 2:j // 2 + 1, Q + (j % 2) * STRIDE:Q + (j % 2) * STRIDE + 1]
                        last = nc.gpsimd.tensor_copy(k[:, :, col:col + 1], src.to_broadcast([C, NQ, 1]))
                    last.then_inc(kt_ready, 1)

                pool.wait_ge(loaded, 96)
                prepare(0, 0)
                keys(0, 0)

                def one(b, half, p):
                    if not (isinstance(b, int) and b == B - 1):
                        prepare(b + 1, 1 - p)
                        keys(b + 1, 1 - p)

                pipelined(pool, B, 2, 2, one)


def route(nc, d, x_sb, pooled):
    NP = B // 2
    GONE = -3.0e38
    with ExitStack() as ctx:
        st = Store(nc, ctx)
        ident = st.sb("ident_r", [128, 128])
        gate_w = st.sb("gate_w", [C, E])
        gate_b = st.sb("gate_b", [2 * E, 1])
        xs = [st.sb(f"xs{p}", [C, L]) for p in range(2)]
        half_neg = st.sb("half_neg_r", [Q, NQ])
        bn = st.sb("bn_r", [Q, NQ, 6])
        mv = st.sb("mv_r", [Q, NQ, 2])
        ve = st.sb("ve", [Q, NQ])
        rs = st.sb("rs", [Q, NQ])
        ln = [st.sb(f"ln_tok{i}", [Q, NQ, C]) for i in range(4)]
        ln_t = st.sb("ln_ch", [C, L])
        lg = st.sb("lg", [2 * E, L])
        ex = st.sb("ex", [2 * E, L])
        wt = st.sb("wt", [2 * E, L])
        wn = [st.sb(f"wn{i}", [2 * E, L]) for i in range(2)]
        wn_t = st.sb("wn_t", [Q, NQ, 2 * E])
        top = st.sb("top", [2 * E, 8])
        sml = st.sb("sml", [2 * E, 4])
        ps_t = [st.ps(f"ps_rt{i}", [128, 512]) for i in range(2)]
        ps_u = [st.ps(f"ps_ru{i}", [128, 512]) for i in range(2)]
        ps_l = [st.ps(f"ps_rl{i}", [128, 512]) for i in range(2)]
        ps_v = st.ps("ps_rv", [128, 512])
        ps_w = st.ps("ps_rw", [128, 512])

        loaded = st.sem("route_loaded")
        waits_apart = st.sem("route_waits_apart")
        xs_loaded = [st.sem(f"xs_loaded{p}") for p in range(2)]
        t1_done = st.sem("t1_done")
        bn_done = st.sem("bn_done")
        ve_ready = st.sem("ve_ready")
        rs_ready = st.sem("rs_ready")
        half_ready = st.sem("half_ready")
        ln_ready = st.sem("ln_tok_ready")
        t2_done = st.sem("t2_done")
        lnt_ready = st.sem("ln_ch_ready")
        lg_done = st.sem("lg_done")
        lg_ready = st.sem("lg_ready")
        top_ready = st.sem("top_ready")
        nmx_ready = st.sem("nmx_ready")
        ex_ready = st.sem("ex_ready")
        gone_ready = st.sem("gone_ready")
        wt_ready = st.sem("wt_ready")
        wn_ready = st.sem("wn_ready")
        wn_saved = st.sem("wn_saved")
        t3_done = st.sem("t3_done")
        wnt_ready = st.sem("wnt_ready")
        pool_done = st.sem("pooled_done")
        pooled_read = st.sem("pooled_read")

        def more(b, n=1):
            return not isinstance(b, int) or b < B - n + 0 * n

        with nc.Block() as block:
            @block.sync
            def _(sp):
                for dst, name in ((ident, "c_ident"), (gate_w, "L1_ffn_gate_w"), (gate_b, "L1_ffn_gate_b")):
                    sp.dma_start(dst[:], d[name]).then_inc(loaded, 16)

                def one(b, half, p):
                    if after(b, 2):
                        sp.wait_ge(t1_done, 2 * b - 2)
                    sp.dma_start(xs[p][:], x_sb[:, bass.ds(b, 1), :].rearrange("c b l -> c (b l)")
                                 ).then_inc(xs_loaded[p], 16)

                pipelined(sp, B, 2, 0, one)
                for p in range(2):
                    sp.wait_ge(xs_loaded[p], 16 * NP)

            def pe_t1(pe, b, half, p):
                pe.wait_ge(xs_loaded[p], 16 * half + 16)
                for h in range(2):
                    if after(b):
                        pe.wait_ge(ln_ready, 2 * b - 1 + h)
                    for i in range(4):
                        j = 4 * h + i
                        last = nc.tensor.transpose(ps_t[h][:, i * C:(i + 1) * C], xs[p][:, j * Q:(j + 1) * Q],
                                                   ident[:])
                    last.then_inc(t1_done, 1)

            def pe_t2(pe, b, p4):
                for h in range(2):
                    pe.wait_ge(ln_ready, 2 * b + 1 + h)
                    if after(b):
                        pe.wait_ge(lnt_ready, 2 * b - 1 + h)
                    for i in range(4):
                        last = nc.tensor.transpose(ps_u[h][:, i * Q:(i + 1) * Q], ln[p4][:, 4 * h + i, :], ident[:])
                    last.then_inc(t2_done, 1)

            def pe_logits(pe, b, half, p):
                if p == 0 and after(half):
                    pe.wait_ge(lg_ready, half)
                for h in range(2):
                    pe.wait_ge(lnt_ready, 2 * b + 1 + h)
                    last = nc.tensor.matmul(ps_l[h][E * p:E * p + E, :], gate_w[:], ln_t[:, h * 512:(h + 1) * 512])
                last.then_inc(lg_done, 1)

            def pe_pool(pe, j, jp):
                pe.wait_ge(wn_ready, j + 1)
                for h in range(2):
                    if h or after(j):
                        pe.wait_ge(wnt_ready, 2 * j + h)
                    for i in range(4):
                        k = 4 * h + i
                        last = nc.tensor.transpose(ps_v[:, i * Q:(i + 1) * Q], wn[jp][:, k * Q:(k + 1) * Q],
                                                   ident[:])
                    last.then_inc(t3_done, 1)
                pe.wait_ge(wnt_ready, 2 * j + 2)
                if after(j):
                    pe.wait_ge(pooled_read, j)
                for q in range(2):
                    for k in range(NQ):
                        last = nc.tensor.matmul(ps_w[:, q * 128:(q + 1) * 128], ln[2 * jp + q][:, k, :],
                                                wn_t[:, k, :], start=(k == 0 and q == 0), stop=(k == NQ - 1),
                                                skip_group_check=True)
                last.then_inc(pool_done, 1)

            def by_pairs(eng, one):
                pipelined(eng, NP, 2, 2, lambda j, half, jp: one(j, jp))

            @block.tensor
            def _(pe):
                pe.wait_ge(loaded, 48)
                pe_t1(pe, 0, 0, 0)

                def one(j, jp):
                    for p in range(2):
                        b = j * 2 + p
                        if not (isinstance(b, int) and b == B - 1):
                            pe_t1(pe, b + 1, j + p, 1 - p)
                        pe_t2(pe, b, 2 * jp + p)
                        pe_logits(pe, b, j, p)
                        if p == 0 and after(j):
                            pe_pool(pe, j - 1, 1 - jp)

                by_pairs(pe, one)
                pe_pool(pe, NP - 1, 1)

            def dve_stats(dve, b):
                for h in range(2):
                    dve.wait_ge(t1_done, 2 * b + 1 + h)
                    for i in range(4):
                        nc.vector.bn_stats(bn[:, 4 * h + i, :], ps_t[h][:, i * C:(i + 1) * C]).then_inc(bn_done, 1)
                dve.wait_ge(bn_done, b * 3 * NQ // 1 + NQ if isinstance(b, int) else b * (3 * NQ) + NQ)
                for i in range(NQ):
                    nc.vector.bn_aggr(mv[:, i, :], bn[:, i, :]).then_inc(bn_done, 2)
                dve.wait_ge(bn_done, b * (3 * NQ) + 3 * NQ)
                nc.vector.tensor_scalar(ve[:], mv[:, :, 1], 1e-5, None, ALU.add).then_inc(ve_ready, 1)

            def dve_norm(dve, b, p4):
                dve.wait_ge(rs_ready, b + 1)
                for h in range(2):
                    for i in range(4 * h, 4 * h + 4):
                        last = nc.vector.tensor_scalar(ln[p4][:, i, :], ps_t[h][:, (i % 4) * C:(i % 4 + 1) * C],
                                                       mv[:, i, 0:1], rs[:, i:i + 1], ALU.subtract, ALU.mult)
                    last.then_inc(ln_ready, 1)

            def dve_top(dve, j):
                dve.wait_ge(lg_ready, j + 1)
                apart(dve, waits_apart)
                nc.vector.max(top[:], lg[:]).then_inc(top_ready, 1)
                dve.wait_ge(top_ready, j + 1)
                if after(j):
                    dve.wait_ge(wn_ready, j)
                apart(dve, waits_apart)
                nc.vector.match_replace(wt[:], top[:], lg[:], GONE).then_inc(gone_ready, 1)

            def dve_weights(dve, j):
                dve.wait_ge(ex_ready, j + 1)
                dve.wait_ge(gone_ready, j + 1)
                nc.vector.reciprocal(sml[:, 2:3], sml[:, 1:2]).then_inc(wt_ready, 1)
                nc.vector.scalar_tensor_tensor(wt[:], wt[:], GONE, ex[:], ALU.is_equal, ALU.mult
                                               ).then_inc(wt_ready, 1)

            @block.vector
            def _(dve):
                dve_stats(dve, 0)
                dve_norm(dve, 0, 0)

                def one(j, jp):
                    for p in range(2):
                        b = j * 2 + p
                        nxt = not (isinstance(b, int) and b == B - 1)
                        if p == 0 and after(j):
                            dve_top(dve, j - 1)
                        if nxt:
                            dve_stats(dve, b + 1)
                        if p == 0 and after(j):
                            dve_weights(dve, j - 1)
                        if nxt:
                            if p == 1 and after(j):
                                dve.wait_ge(pool_done, j)
                            dve_norm(dve, b + 1, (2 * jp + p + 1) % 4)

                by_pairs(dve, one)
                dve_top(dve, NP - 1)
                dve_weights(dve, NP - 1)

            def act_lnt(act, b):
                for h in range(2):
                    act.wait_ge(t2_done, 2 * b + 1 + h)
                    if h == 0 and after(b):
                        act.wait_ge(lg_done, b)
                    nc.scalar.copy(ln_t[:, h * 512:(h + 1) * 512], ps_u[h][:]).then_inc(lnt_ready, 1)

            def act_logits(act, j):
                act.wait_ge(lg_done, 2 * j + 2)
                if after(j):
                    act.wait_ge(gone_ready, j)
                nc.scalar.activation(lg[:, 0:512], ps_l[0][:], ACT_ID, bias=gate_b[:, 0:1])
                nc.scalar.activation(lg[:, 512:], ps_l[1][:], ACT_ID, bias=gate_b[:, 0:1]).then_inc(lg_ready, 1)

            def act_exp(act, j):
                act.wait_ge(top_ready, j + 1)
                if after(j):
                    act.wait_ge(wt_ready, 2 * j)
                nc.scalar.mul(sml[:, 0:1], top[:, 0:1], -1.0).then_inc(nmx_ready, 1)
                act.wait_ge(nmx_ready, j + 1)
                nc.scalar.activation(ex[:], lg[:], ACT.Exp, bias=sml[:, 0:1], accum_out=sml[:, 1:2]
                                     ).then_inc(ex_ready, 1)

            def act_weights(act, j, jp):
                act.wait_ge(wt_ready, 2 * j + 2)
                if after(j, 2):
                    act.wait_ge(wn_saved, 16 * j - 16)
                    act.wait_ge(t3_done, 2 * j - 2)
                nc.scalar.mul(wn[jp][:], wt[:], sml[:, 2:3]).then_inc(wn_ready, 1)

            def act_pool(act, j):
                for h in range(2):
                    act.wait_ge(t3_done, 2 * j + 1 + h)
                    if h == 0 and after(j):
                        act.wait_ge(pool_done, j)
                    nc.scalar.copy(wn_t[:, 4 * h:4 * h + 4, :], ps_v[:].rearrange("q (i e) -> q i e", e=2 * E)
                                   ).then_inc(wnt_ready, 1)
                act.wait_ge(pool_done, j + 1)
                for q in range(2):
                    last = nc.scalar.copy(pooled[:, :, bass.ds(j * 2 + q, 1)].rearrange("c e b -> c (e b)"),
                                          ps_w[:, q * (128 + E):q * (128 + E) + E])
                last.then_inc(pooled_read, 1)

            @block.scalar
            def _(act):
                act.wait_ge(loaded, 48)

                def one(j, jp):
                    for p in range(2):
                        b = j * 2 + p
                        act_lnt(act, b)
                        if p == 0 and after(j):
                            act_exp(act, j - 1)
                            act_weights(act, j - 1, 1 - jp)
                            act_pool(act, j - 1)
                    act_logits(act, j)

                by_pairs(act, one)
                act_exp(act, NP - 1)
                act_weights(act, NP - 1, 1)
                act_pool(act, NP - 1)

            @block.gpsimd
            def _(pool):
                nc.gpsimd.memset(half_neg[:], -0.5).then_inc(half_ready, 1)
                pool.wait_ge(half_ready, 1)

                def saved(j, jp):
                    pool.wait_ge(wn_ready, j + 1)
                    if after(j):
                        pool.wait_ge(wn_saved, 16 * j)
                    pool.dma_start(d["s_wn"][bass.ds(j, 1)].rearrange("j e l -> (j e) l"), wn[jp][:]
                                   ).then_inc(wn_saved, 16)

                def rstd(b):
                    pool.wait_ge(ve_ready, b + 1)
                    nc.gpsimd.tensor_tensor(rs[:], ve[:], half_neg[:], ALU.pow).then_inc(rs_ready, 1)

                rstd(0)

                def one(j, jp):
                    for p in range(2):
                        b = j * 2 + p
                        if not (isinstance(b, int) and b == B - 1):
                            rstd(b + 1)
                        if p == 0 and after(j):
                            saved(j - 1, 1 - jp)

                by_pairs(pool, one)
                saved(NP - 1, 1)
                pool.wait_ge(wn_saved, 16 * NP)


def experts(nc, d, pooled):
    G = 4
    NGRP = E // G
    with ExitStack() as ctx:
        st = Store(nc, ctx)
        ident = st.sb("ident_e", [128, 128])
        ones = st.sb("ones_e", [1, B])
        w1 = [st.sb(f"w1_{i}", [C, G, H]) for i in range(2)]
        b1 = [st.sb(f"b1_{i}", [1, G, H]) for i in range(2)]
        w2 = [st.sb(f"w2_{i}", [128, G, KE, C]) for i in range(2)]
        b2 = [st.sb(f"b2_{i}", [1, G, C]) for i in range(2)]
        xe = [st.sb(f"xe{i}", [C, G, B]) for i in range(2)]
        he = st.sb("he", [128, H])
        he_t = st.sb("he_t", [128, KE, 128])
        oe = [st.sb(f"oe{i}", [128, C]) for i in range(2)]
        ps_h = [st.ps(f"ps_eh{i}", [128, H]) for i in range(2)]
        ps_t = st.ps("ps_et", [128, KE, 128])
        ps_o = [st.ps(f"ps_eo{i}", [128, 512]) for i in range(2)]
        loaded = st.sem("experts_loaded")
        waits_apart = st.sem("experts_waits_apart")
        ones_ready = st.sem("ones_ready")
        w_loaded = [st.sem(f"expert_w_loaded{i}") for i in range(2)]
        xe_ready = st.sem("xe_ready")
        h_done = st.sem("eh_done")
        he_ready = st.sem("he_ready")
        t_done = st.sem("et_done")
        het_ready = st.sem("het_ready")
        o_done = st.sem("eo_done")
        oe_ready = st.sem("oe_ready")
        oe_saved = st.sem("oe_saved")

        with nc.Block() as block:
            @block.sync
            def _(sp):
                sp.dma_start(ident[:], d["c_ident"]).then_inc(loaded, 16)

                def one(g, half, p):
                    if after(g, 2):
                        sp.wait_ge(o_done, g - 1)
                    e = bass.ds(g * G, G)
                    sp.dma_start(w1[p][:], d["w1"][e, 0:C, :].rearrange("e c h -> c e h")).then_inc(w_loaded[p], 16)
                    sp.dma_start(b1[p][:], d["w1"][e, C:C + 1, :].rearrange("e c h -> c e h")
                                 ).then_inc(w_loaded[p], 16)
                    sp.dma_start(w2[p][:], d["w2"][e, 0:H, :].rearrange("e (q j) o -> q e (j o)", j=KE)
                                 ).then_inc(w_loaded[p], 16)
                    sp.dma_start(b2[p][:], d["w2"][e, H:H + 1, :].rearrange("e h o -> h e o")
                                 ).then_inc(w_loaded[p], 16)

                pipelined(sp, NGRP, 2, 0, one)

            @block.tensor
            def _(pe):
                pe.wait_ge(loaded, 16)
                pe.wait_ge(ones_ready, 1)

                def one(g, half, p):
                    pe.wait_ge(w_loaded[p], 64 * half + 64)
                    pe.wait_ge(xe_ready, g + 1)
                    if after(g, 2):
                        pe.wait_ge(he_ready, g - 1)
                    for c in range(G):
                        nc.tensor.matmul(ps_h[p][32 * c:32 * c + 32, :], xe[p][:, c, :], w1[p][:, c, :],
                                         start=True, stop=False, skip_group_check=True)
                    for c in range(G):
                        last = nc.tensor.matmul(ps_h[p][32 * c:32 * c + 32, :], ones[:], b1[p][:, c, :],
                                                start=False, stop=True, skip_group_check=True,
                                                tile_position=(0, 32 * c))
                    last.then_inc(h_done, 1)
                    pe.wait_ge(he_ready, g + 1)
                    if after(g):
                        pe.wait_ge(het_ready, g)
                    for j in range(KE):
                        last = nc.tensor.transpose(ps_t[:, j, :], he[:].rearrange("q (a j) -> q j a", j=KE)[:, j, :],
                                                   ident[:])
                    last.then_inc(t_done, 1)
                    pe.wait_ge(het_ready, g + 1)
                    if after(g, 2):
                        pe.wait_ge(oe_ready, g - 1)
                    for j in range(KE):
                        for c in range(G):
                            nc.tensor.matmul(ps_o[p][32 * c:32 * c + 32, 0:C], he_t[:, j, 32 * c:32 * c + 32],
                                             w2[p][:, c, j, :], start=(j == 0), stop=False, skip_group_check=True)
                    for c in range(G):
                        last = nc.tensor.matmul(ps_o[p][32 * c:32 * c + 32, 0:C], ones[:], b2[p][:, c, :],
                                                start=False, stop=True, skip_group_check=True,
                                                tile_position=(0, 32 * c))
                    last.then_inc(o_done, 1)

                pipelined(pe, NGRP, 2, 0, one)

            @block.gpsimd
            def _(pool):
                def one(g, half, p):
                    if after(g, 2):
                        pool.wait_ge(h_done, g - 1)
                    apart(pool, waits_apart)
                    nc.gpsimd.tensor_copy(xe[p][:], pooled[:, bass.ds(g * G, G), :]).then_inc(xe_ready, 1)

                pipelined(pool, NGRP, 2, 0, one)

            @block.scalar
            def _(act):
                def one(g, half, p):
                    act.wait_ge(h_done, g + 1)
                    if after(g):
                        act.wait_ge(t_done, g)
                    nc.scalar.activation(he[:], ps_h[p][:], ACT.Gelu).then_inc(he_ready, 1)
                    act.wait_ge(oe_ready, g + 1)
                    if after(g):
                        act.wait_ge(oe_saved, 64 * g)
                    for c in range(G):
                        act.dma_start(d["s_oe"][:, bass.ds(g * G + c, 1), :].rearrange("b e o -> b (e o)"),
                                      oe[p][32 * c:32 * c + 32, :]).then_inc(oe_saved, 16)

                pipelined(act, NGRP, 2, 0, one)
                act.wait_ge(oe_saved, 64 * NGRP)

            @block.vector
            def _(dve):
                nc.vector.memset(ones[:], 1.0).then_inc(ones_ready, 1)

                def one(g, half, p):
                    dve.wait_ge(t_done, g + 1)
                    if after(g):
                        dve.wait_ge(o_done, g)
                    nc.vector.tensor_copy(he_t[:], ps_t[:]).then_inc(het_ready, 1)
                    dve.wait_ge(o_done, g + 1)
                    if after(g, 2):
                        dve.wait_ge(oe_saved, 64 * g - 64)
                    nc.vector.tensor_copy(oe[p][:], ps_o[p][:, 0:C]).then_inc(oe_ready, 1)

                pipelined(dve, NGRP, 2, 0, one)


def combine(nc, d, x_sb, out):
    NP = B // 2
    with ExitStack() as ctx:
        st = Store(nc, ctx)
        wn = [st.sb(f"wn_c{i}", [2 * E, L]) for i in range(2)]
        oe = [st.sb(f"oe_c{i}", [2 * E, C]) for i in range(2)]
        ps = [st.ps(f"ps_c{i}", [128, 512]) for i in range(8)]
        in_loaded = [st.sem(f"in_loaded{i}") for i in range(2)]
        mm_done = st.sem("mm_done")
        added = st.sem("added")
        stored = st.sem("stored")

        with nc.Block() as block:
            @block.scalar
            def _(act):
                def one(j, half, jp):
                    if after(j, 2):
                        act.wait_ge(mm_done, 4 * j - 4)
                    act.dma_start(wn[jp][:], d["s_wn"][bass.ds(j, 1)].rearrange("j e l -> (j e) l")
                                  ).then_inc(in_loaded[jp], 16)
                    act.dma_start(oe[jp][:], d["s_oe"][bass.ds(j * 2, 2)].rearrange("b e o -> (b e) o")
                                  ).then_inc(in_loaded[jp], 16)

                pipelined(act, NP, 2, 0, one)

            @block.tensor
            def _(pe):
                def one(j, half, jp):
                    pe.wait_ge(in_loaded[jp], 32 * half + 32)
                    for q in range(2):
                        for h in range(2):
                            k = 2 * q + h
                            if after(j, 2):
                                pe.wait_ge(added, 4 * j + k - 7)
                            nc.tensor.matmul(ps[4 * jp + k][:], oe[jp][E * q:E * q + E, :],
                                             wn[jp][E * q:E * q + E, h * 512:(h + 1) * 512]).then_inc(mm_done, 1)

                pipelined(pe, NP, 2, 0, one)

            @block.vector
            def _(dve):
                def one(j, half, jp):
                    for q in range(2):
                        for h in range(2):
                            k = 2 * q + h
                            dve.wait_ge(mm_done, 4 * j + k + 1)
                            xs = x_sb[:, bass.ds(j * 2 + q, 1), h * 512:(h + 1) * 512].rearrange("c b l -> c (b l)")
                            nc.vector.tensor_tensor(xs, ps[4 * jp + k][:], xs, ALU.add).then_inc(added, 1)

                pipelined(dve, NP, 2, 0, one)

            @block.sync
            def _(sp):
                with sp.Fori(0, B) as b:
                    sp.wait_ge(added, b * 2 + 2)
                    sp.dma_start(out[bass.ds(b, 1)].rearrange("b c l -> c (b l)"),
                                 x_sb[:, bass.ds(b, 1), :].rearrange("c b l -> c (b l)")).then_inc(stored, 16)
                sp.wait_ge(stored, 16 * B)


def build(nc, d, out):
    with ExitStack() as ctx:
        st = Store(nc, ctx)
        x_sb = st.sb("x_sb", [C, B, L])
        with ExitStack() as ctx1:
            s1 = Store(nc, ctx1)
            mask = s1.sb("mask", [Q, NQ, 2 * Q + NG])
            wvo = s1.sb("wvo", [C, C])
            bvo = s1.sb("bvo", [C, C])
            with ExitStack() as ctx2:
                s2 = Store(nc, ctx2)
                ln_r = s2.sb("ln_r", [B, L])
                ln_mr = s2.sb("ln_mr", [B, L])
                spikes = s2.sb("spikes", [B, L])
                scale_cb = s2.sb("scale_cb", [C, B])
                shift_cb = s2.sb("shift_cb", [C, B])
                load_and_norm(nc, d, x_sb, scale_cb, shift_cb)
                rnn_layer(nc, d, x_sb, scale_cb, shift_cb, ln_r, ln_mr, spikes)
                build_mask(nc, d, spikes, ln_r, ln_mr, mask, wvo, bvo)
            attention(nc, d, x_sb, mask, wvo, bvo)
        pooled = st.sb("pooled", [C, E, B])
        route(nc, d, x_sb, pooled)
        experts(nc, d, pooled)
        combine(nc, d, x_sb, out)


def kernel(**inputs):
    import numpy as np
    import concourse.bacc as bacc
    from concourse.bass_utils import run_bass_kernel_spmd

    f = {k: np.asarray(v) for k, v in inputs.items()}

    def rows(w, k):
        return w.reshape(k, 128, -1).transpose(1, 0, 2)

    ch = np.arange(C)
    q, n = np.arange(Q)[:, None], np.arange(Q)[None, :]
    a = {
        "x": f["x"].reshape(B, C, L),
        "L0_conv_gamma": f["L0_conv_gamma"][:, None],
        "L0_conv_beta": f["L0_conv_beta"][:, None],
        "L0_conv_w_in": f["L0_conv_w_in"].T,
        "L0_conv_b_in": f["L0_conv_b_in"].reshape(KI, 128).T,
        "L0_conv_w_ih": rows(f["L0_conv_w_ih"].T, KI),
        "L0_conv_b_ih": f["L0_conv_b_ih"].reshape(KH, 128).T,
        "L0_conv_w_hh": rows(f["L0_conv_w_hh"].T, KH),
        "L0_conv_b_hh": f["L0_conv_b_hh"].reshape(KH, 128).T,
        "L0_conv_w_out": rows(f["L0_conv_w_out"].T, KH),
        "L0_conv_b_out": f["L0_conv_b_out"][:, None],
        "L1_attn_Ws": f["L1_attn_Ws"],
        "L1_attn_bs": f["L1_attn_bs"],
        "L1_attn_Wq": f["L1_attn_Wq"],
        "L1_attn_Wk": f["L1_attn_Wk"],
        "L1_attn_Wv": f["L1_attn_Wv"].T,
        "L1_attn_Wo": f["L1_attn_Wo"],
        "L1_attn_bq": f["L1_attn_bq"][:, None],
        "L1_attn_bk": f["L1_attn_bk"][:, None],
        "L1_attn_bv": f["L1_attn_bv"][:, None],
        "L1_attn_bo": f["L1_attn_bo"][:, None],
        "L1_ffn_gate_w": f["L1_ffn_gate_w"].T,
        "L1_ffn_gate_b": np.concatenate([f["L1_ffn_gate_b"]] * 2)[:, None],
        "w1": f["L1_ffn_weight1"],
        "w2": f["L1_ffn_weight2"],
        "c_group_mean": (ch[:, None] // (C // GROUPS) == ch[None, :] // (C // GROUPS)).astype(np.float32)
        / (C // GROUPS),
        "c_mean": np.full((C, C), 1.0 / C, np.float32),
        "c_ident": np.eye(128, dtype=np.float32),
        "c_tri": np.concatenate([np.where(n >= q, 0.0, NEG), np.where(n <= q, 0.0, NEG)], 1).astype(np.float32),
    }
    nc = bacc.Bacc("TRN2", target_bir_lowering=False, num_devices=1)
    arrays, d = {}, {}
    for name, v in a.items():
        arrays["in_" + name] = np.ascontiguousarray(v)
        d[name] = nc.dram_tensor("in_" + name, v.shape, F32, kind="ExternalInput").ap()
    out = nc.dram_tensor("out_y", (B, C, L), F32, kind="ExternalOutput").ap()
    d["s_ln"] = nc.dram_tensor("s_ln", (2, B, L), F32, kind="Internal").ap()
    d["s_wn"] = nc.dram_tensor("s_wn", (B // 2, 2 * E, L), F32, kind="Internal").ap()
    d["s_oe"] = nc.dram_tensor("s_oe", (B, E, C), F32, kind="Internal").ap()
    build(nc, d, out)
    r = run_bass_kernel_spmd(nc, [arrays], core_ids=[0])
    return r.results[0]["out_y"].reshape(B, C, 32, 32)
```

```python
from contextlib import ExitStack

import concourse.bass as bass
from concourse import mybir
from concourse.alu_op_type import AluOpType as ALU

F32 = mybir.dt.float32
F16 = mybir.dt.float16
I32 = mybir.dt.int32
ACT = mybir.ActivationFunctionType
AX_X = mybir.AxisListType.X

B, C, L = 32, 128, 1024
GROUPS = 32
RIN, RH = 256, 512
KI, KH = RIN // 128, RH // 128
T = 8
NBLK = L // T
E, H, TOPK = 64, 512, 8
KE = H // 128
Q = 128
NQ = L // Q
WINDOW, STRIDE, FIRST = 128, 64, 4
NG = FIRST + L // STRIDE - 1
W_TOP = 2.0 ** 14
BN_MAX = 182.0
LO_SCALE = 2.0 ** 12
NEG = -1.0e30
DECAY = 0.9048374180359595
SCALE = 1.0 / C ** 0.5
ACT_ID = ACT.Identity


class Chain:

    def __init__(self, eng, sem, base=0):
        self.eng, self.sem, self.base, self.n = eng, sem, base, 0

    def step(self, ins):
        self.n += 1
        ins.then_inc(self.sem, 1)
        self.eng.wait_ge(self.sem, self.base + self.n)


class Store:

    def __init__(self, nc, ctx):
        self.nc, self.ctx = nc, ctx

    def sb(self, name, shape, dt=F32):
        t = self.ctx.enter_context(self.nc.sbuf_tensor(name, shape, dt))
        return t

    def ps(self, name, shape, dt=F32):
        return self.ctx.enter_context(self.nc.psum_tensor(name, shape, dt))

    def sem(self, name):
        return self.ctx.enter_context(self.nc.semaphore(name))


def load_and_norm(nc, d, x_sb, scale_cb, shift_cb):
    NLOAD = 8
    PER = B // NLOAD
    with ExitStack() as ctx:
        st = Store(nc, ctx)
        stats = st.sb("stats", [C, B, 2, 6])
        moments = st.sb("moments", [C, 2, B])
        mv = st.sb("mv", [C, B, 2])
        group_mean = st.sb("group_mean", [C, C])
        gn = st.sb("gn", [C, 2, B])
        t1 = st.sb("t1", [C, B])
        t2 = st.sb("t2", [C, B])
        gr = st.sb("gr", [C, B])
        vm = st.sb("vm", [C, B])
        e2 = st.sb("e2", [C, B])
        bn = st.sb("bn", [C, 8])
        gamma = st.sb("gamma", [C, 1])
        beta = st.sb("beta", [C, 1])
        half_neg = st.sb("half_neg", [C, B])
        ps_gn = st.ps("ps_gn", [C, 2, B])
        x_loaded = [st.sem(f"x_loaded{i}") for i in range(NLOAD)]
        params_loaded = st.sem("params_loaded")
        dve_step = st.sem("dve_step")
        stats_done = st.sem("stats_done")
        moments_ready = st.sem("moments_ready")
        group_ready = st.sem("group_ready")
        var_ready = st.sem("var_ready")
        rstd_ready = st.sem("rstd_ready")
        pow_ready = st.sem("pow_ready")
        xd = d["x"]

        with nc.Block() as block:
            @block.sync
            def _(sp):
                sp.dma_start(group_mean[:], d["c_group_mean"]).then_inc(params_loaded, 16)
                sp.dma_start(gamma[:], d["L0_conv_gamma"]).then_inc(params_loaded, 16)
                sp.dma_start(beta[:], d["L0_conv_beta"]).then_inc(params_loaded, 16)
                for i in range(NLOAD):
                    sp.dma_start(x_sb[:, i * PER:(i + 1) * PER, :],
                                 xd[i * PER:(i + 1) * PER].rearrange("b c l -> c b l")).then_inc(x_loaded[i], 16)

            @block.tensor
            def _(pe):
                pe.wait_ge(params_loaded, 48)
                pe.wait_ge(moments_ready, 2)
                nc.tensor.matmul(ps_gn[:].rearrange("p a b -> p (a b)"), group_mean[:],
                                 moments[:].rearrange("p a b -> p (a b)")).then_inc(group_ready, 1)

            @block.gpsimd
            def _(pool):
                nc.gpsimd.memset(half_neg[:], -0.5).then_inc(pow_ready, 1)
                pool.wait_ge(pow_ready, 1)
                pool.wait_ge(var_ready, 1)
                nc.gpsimd.tensor_tensor(gr[:], t2[:], half_neg[:], ALU.pow).then_inc(rstd_ready, 1)
                pool.wait_ge(var_ready, 2)
                nc.gpsimd.tensor_tensor(bn[:, 3:4], bn[:, 2:3], half_neg[:, 0:1], ALU.pow).then_inc(rstd_ready, 1)

            @block.vector
            def _(dve):
                v = nc.vector
                for i in range(NLOAD):
                    dve.wait_ge(x_loaded[i], 16)
                    with dve.Fori(i * PER, (i + 1) * PER) as b:
                        for h in range(2):
                            v.bn_stats(stats[:, bass.ds(b, 1), h, :].rearrange("p b s -> p (b s)"),
                                       x_sb[:, bass.ds(b, 1), h * 512:(h + 1) * 512].rearrange("p b l -> p (b l)")
                                       ).then_inc(stats_done, 1)
                dve.wait_ge(stats_done, 2 * B)
                for b in range(B):
                    last = v.bn_aggr(mv[:, b, :], stats[:, b])
                    last.then_inc(stats_done, 1)
                dve.wait_ge(stats_done, 3 * B)
                ch = Chain(dve, dve_step)
                v.tensor_copy(moments[:, 0, :], mv[:, :, 0]).then_inc(moments_ready, 1)
                ch.step(v.tensor_tensor(t1[:], mv[:, :, 0], mv[:, :, 0], ALU.mult))
                v.tensor_tensor(moments[:, 1, :], t1[:], mv[:, :, 1], ALU.add).then_inc(moments_ready, 1)
                dve.wait_ge(group_ready, 1)
                ch.step(v.tensor_copy(gn[:], ps_gn[:]))
                ch.step(v.tensor_tensor(t1[:], gn[:, 0, :], gn[:, 0, :], ALU.mult))
                ch.step(v.tensor_tensor(t1[:], gn[:, 1, :], t1[:], ALU.subtract))
                v.tensor_scalar(t2[:], t1[:], 1e-5, None, ALU.add).then_inc(var_ready, 1)
                dve.wait_ge(rstd_ready, 1)
                ch.step(v.tensor_tensor(t1[:], mv[:, :, 0], gn[:, 0, :], ALU.subtract))
                ch.step(v.tensor_tensor(vm[:], t1[:], gr[:], ALU.mult))
                ch.step(v.tensor_tensor(t1[:], gr[:], gr[:], ALU.mult))
                ch.step(v.tensor_tensor(t1[:], t1[:], mv[:, :, 1], ALU.mult))
                ch.step(v.tensor_reduce(bn[:, 0:1], vm[:], AX_X, ALU.add))
                ch.step(v.tensor_scalar(bn[:, 1:2], bn[:, 0:1], 1.0 / B, None, ALU.mult))
                ch.step(v.tensor_scalar(t2[:], vm[:], bn[:, 1:2], None, ALU.subtract))
                ch.step(v.tensor_tensor(t2[:], t2[:], t2[:], ALU.mult))
                ch.step(v.tensor_tensor(e2[:], t1[:], t2[:], ALU.add))
                ch.step(v.tensor_reduce(bn[:, 4:5], e2[:], AX_X, ALU.add))
                v.tensor_scalar(bn[:, 2:3], bn[:, 4:5], 1.0 / B, 1e-5, ALU.mult, ALU.add).then_inc(var_ready, 1)
                dve.wait_ge(rstd_ready, 2)
                dve.wait_ge(params_loaded, 48)
                ch.step(v.tensor_tensor(bn[:, 5:6], bn[:, 3:4], gamma[:], ALU.mult))
                ch.step(v.tensor_scalar(scale_cb[:], gr[:], bn[:, 5:6], None, ALU.mult))
                ch.step(v.tensor_tensor(t1[:], gn[:, 0, :], gr[:], ALU.mult))
                ch.step(v.tensor_scalar(t1[:], t1[:], bn[:, 1:2], bn[:, 5:6], ALU.add, ALU.mult))
                ch.step(v.tensor_scalar(shift_cb[:], t1[:], -1.0, beta[:, 0:1], ALU.mult, ALU.add))


def rnn_layer(nc, d, x_sb, scale_cb, shift_cb, ln_r, ln_mr, spikes):
    with ExitStack() as ctx:
        st = Store(nc, ctx)
        w_in = st.sb("w_in", [C, RIN])
        i_hi = st.sb("i_hi", [128, KI, RH], F16)
        i_lo = st.sb("i_lo", [128, KI, RH], F16)
        xg_all = st.sb("xg_all", [128, 2, T, KH, B])
        w_hh = xg_all[:].rearrange("p a t k b -> p (a t k b)").rearrange("p (k m) -> p k m", k=KH)
        b_in = st.sb("b_in", [128, KI])
        b_ih = st.sb("b_ih", [128, KH])
        b_hh = st.sb("b_hh", [128, KH])
        b_g = st.sb("b_g", [128, KH])
        b_out = st.sb("b_out", [C, 1])
        stat_w = st.sb("stat_w", [C, 2, 32])
        ws = st.sb("ws", [C, 1])
        bs = st.sb("bs", [B, 1])
        mean_w = st.sb("mean_w", [C, C])
        w_abs = st.sb("w_abs", [128, 4, 4])
        w_scale = st.sb("w_scale", [128, 2, 4])
        xg_undo = st.sb("xg_undo", [128, 1])
        gb = st.sb("gb", [C, 2])
        gb_abs = st.sb("gb_abs", [C, 2])
        xn_max = st.sb("xn_max", [C, 1])
        z_max = st.sb("z_max", [128, KI])
        b_abs = st.sb("b_abs", [128, KI])
        w_hi = st.sb("w_hi", [128, KH, RH], F16)
        w_lo = st.sb("w_lo", [128, KH, RH], F16)
        w_hi_s = st.sb("w_hi_s", [128, KH, RH], F16)
        o_hi = st.sb("o_hi", [128, KH, C], F16)
        o_lo = st.sb("o_lo", [128, KH, C], F16)
        o_hi_s = st.sb("o_hi_s", [128, KH, C], F16)
        ws_c = st.sb("ws_c", [C, 1])
        h_parts = st.sb("h_parts", [128, 2, 2, KH, T, B], F16)
        h_hi = [h_parts[:, p, 0] for p in range(2)]
        h_lo = [h_parts[:, p, 1] for p in range(2)]
        w_ih = h_parts[:, 0].rearrange("q a k t b -> q (a k t b)").bitcast(F32).rearrange("q (k m) -> q k m", k=KI)
        h = [st.sb(f"h_{s}", [128, 2, B]) for s in "ab"]
        hi4 = [st.sb(f"hi4_{s}", [128, 2, B], F16) for s in "ab"]
        xg = [xg_all[:, p] for p in range(2)]
        pre = [[st.sb(f"pre{s}{i}", [128, 2, B]) for i in range(2)] for s in "ab"]
        xn = st.sb("xn", [C, T, B])
        xn_s = st.sb("xn_s", [C, T, B])
        tz = st.sb("tz", [128, KI, T * B])
        w_out = tz[:].rearrange("p k n -> p (k n)").rearrange("p (k m) -> p k m", k=KH)
        inp = st.sb("inp", [128, KI, T * B])
        inp_hi = st.sb("inp_hi", [128, KI, T * B], F16)
        inp_lo = st.sb("inp_lo", [128, KI, T * B], F16)
        yb = st.sb("yb", [C, T, B])
        y = st.sb("y", [C, T, B])
        ysq = st.sb("ysq", [C, T, B])
        rows = st.sb("rows", [96, B, T])
        sm = st.sb("sm", [B, 3, T])
        ln_t = st.sb("ln_t", [B, 5, T])
        one8 = st.sb("one8", [B, T])
        cur = [st.sb(f"cur{p}", [B, T]) for p in range(2)]
        half_neg = st.sb("half_neg2", [B, T])
        mem = st.sb("mem", [B, 1])
        memp = st.sb("memp", [B, T])

        ps_h = [[st.ps(f"ps_h{s}{i}", [128, 512]) for i in range(2)] for s in "ab"]
        ps_xg = [st.ps(f"ps_xg{i}", [128, 2, T * B]) for i in range(2)]
        ps_z = st.ps("ps_z", [128, KI, T * B])
        ps_y = st.ps("ps_y", [128, 512])

        loaded = st.sem("rnn_loaded")
        setup = st.sem("rnn_setup")
        mean_ready = st.sem("mean_ready")
        psum_ready = [st.sem(f"psum_ready_{s}") for s in "ab"]
        pre_ready = [st.sem(f"pre_ready_{s}") for s in "ab"]
        hi_ready = [st.sem(f"hi_ready_{s}") for s in "ab"]
        h_ready = st.sem("h_ready")
        hi4_ready = [st.sem(f"hi4_ready_{s}") for s in "ab"]
        lo_ready = [st.sem(f"lo_ready_{s}") for s in "ab"]
        w_step = st.sem("w_step")
        w_max = st.sem("w_max")
        rows_ready = st.sem("rows_ready")
        rows_moved = st.sem("rows_moved")
        xn_step = st.sem("xn_step")
        xn_ready = st.sem("xn_ready")
        z_ready = st.sem("z_ready")
        tz_ready = st.sem("tz_ready")
        inp_ready = st.sem("inp_ready")
        ihi_ready = st.sem("ihi_ready")
        ilo_ready = st.sem("ilo_ready")
        bound_step = st.sem("bound_step")
        xgp_ready = st.sem("xgp_ready")
        xg_ready = st.sem("xg_ready")
        yp_ready = st.sem("yp_ready")
        yb_ready = st.sem("yb_ready")
        y_ready = st.sem("y_ready")
        ysq_ready = st.sem("ysq_ready")
        stp_ready = st.sem("stp_ready")
        var_ready = st.sem("var_ready")
        sm_ready = st.sem("sm_ready")
        ln_step = st.sem("ln_step")
        cur_ready = st.sem("cur_ready")
        memp_ready = st.sem("memp_ready")
        mem_ready = st.sem("mem_ready")

        NLOADS = 13
        SETUP = 12
        HI_STEP = 6

        def tokens(g):
            return x_sb[:, :, bass.ds(g * T, T)].rearrange("c b l -> c l b")

        with nc.Block() as block:
            @block.sync
            def _(sp):
                for dst, name in ((w_hh, "L0_conv_w_hh"), (w_ih, "L0_conv_w_ih"), (w_out, "L0_conv_w_out"),
                                  (mean_w[:], "c_mean")):
                    sp.dma_start(dst, d[name]).then_inc(loaded, 16)

                def move(g):
                    sp.wait_ge(rows_ready, g + 1)
                    if not isinstance(g, int) or g > 0:
                        sp.wait_ge(cur_ready, g)
                    for i in range(3):
                        sp.dma_start(sm[:, i, :], rows[32 * i:32 * i + 1, :, :]
                                     ).then_inc(rows_moved, 16)

                move(0)
                with sp.Fori(1, NBLK) as g:
                    move(g)
                sp.wait_ge(rows_moved, 48 * NBLK)

            def pe_inproj(pe, g):
                pe.wait_ge(xn_ready, g + 1)
                if not isinstance(g, int) or g > 0:
                    pe.wait_ge(inp_ready, g)
                for m in range(KI):
                    last = nc.tensor.matmul(ps_z[:, m, :], w_in[:, m * 128:(m + 1) * 128],
                                            xn[:].rearrange("c t b -> c (t b)"), start=(m == 0), stop=True,
                                            skip_group_check=True)
                last.then_inc(z_ready, 1)

            def pe_xgate(pe, g, m):
                if m == 0:
                    pe.wait_ge(ilo_ready, g + 1)
                if m % 2 == 0 and after(g):
                    pe.wait_ge(xg_ready, 2 * g - 1 + m // 2)
                for k in range(KI):
                    for n, (w, x) in enumerate(((i_hi, inp_hi), (i_lo, inp_hi), (i_hi, inp_lo))):
                        last = nc.tensor.matmul(ps_xg[m // 2][:, m % 2, :], w[:, k, m * 128:(m + 1) * 128],
                                                x[:, k, :], start=(m % 2 == 0 and k == 0 and n == 0),
                                                stop=(k == KI - 1 and n == 2), skip_group_check=True)
                if m % 2 == 1:
                    last.then_inc(xgp_ready, 1)

            def pe_yproj(pe, g, p, half):
                if half == 0 and after(g):
                    pe.wait_ge(rows_ready, g)
                for k in (2 * half, 2 * half + 1):
                    for n, (w, hx) in enumerate(((o_hi, h_hi), (o_lo, h_hi), (o_hi_s, h_lo))):
                        last = nc.tensor.matmul(ps_y[:, 0:T * B], w[:, k, :],
                                                hx[p][:, k].rearrange("q t b -> q (t b)"),
                                                start=(k == 0 and n == 0), stop=(k == KH - 1 and n == 2),
                                                skip_group_check=True)
                if half == 1:
                    last.then_inc(yp_ready, 1)

            def pe_stats(pe, g):
                pe.wait_ge(y_ready, g + 1)
                for i in range(2):
                    nc.tensor.matmul(ps_y[32 * i:32 * i + 32, 0:T * B], stat_w[:, i, :],
                                     y[:].rearrange("c t b -> c (t b)"), start=True, stop=True)
                pe.wait_ge(ysq_ready, g + 1)
                nc.tensor.matmul(ps_y[64:96, 0:T * B], stat_w[:, 0, :], ysq[:].rearrange("c t b -> c (t b)"),
                                 start=True, stop=True).then_inc(stp_ready, 1)

            def pe_block(pe, g, p, ahead1=True, ahead2=True, behind=True):
                for s in range(T):
                    i = s % 2
                    q, r = (p, s - 1) if s else (1 - p, T - 1)

                    def mm(half, ks, w, hx, first=False, last=False):
                        for k in ks:
                            for m in (2 * half, 2 * half + 1):
                                ins = nc.tensor.matmul(ps_h[half][i][:, (m % 2) * B:(m % 2 + 1) * B],
                                                       w[:, k, m * 128:(m + 1) * 128], hx[q][:, k, r, :],
                                                       start=(first and k == 0 and m % 2 == 0), stop=last,
                                                       skip_group_check=True)
                        if last:
                            ins.then_inc(psum_ready[half], 1)

                    first_ks, last_ks = (0, 1), (2, 3)
                    pe.wait_ge(hi_ready[0], g * T + s + 1)
                    for half in range(2):
                        mm(half, first_ks, w_hi, h_hi, first=True)
                        mm(half, first_ks, w_lo, h_hi)
                    pe.wait_ge(hi_ready[1], g * T + s + 1)
                    mm(0, last_ks, w_hi, h_hi)
                    mm(0, last_ks, w_lo, h_hi)
                    pe.wait_ge(lo_ready[0], g * T + s + 1)
                    mm(0, first_ks, w_hi_s, h_lo)
                    mm(1, first_ks, w_hi_s, h_lo)
                    pe.wait_ge(lo_ready[1], g * T + s + 1)
                    mm(0, last_ks, w_hi_s, h_lo, last=True)
                    mm(1, last_ks, w_hi, h_hi)
                    mm(1, last_ks, w_lo, h_hi)
                    mm(1, last_ks, w_hi_s, h_lo, last=True)
                    if s in (0, 1) and behind:
                        pe_yproj(pe, g - 1, 1 - p, s)
                    if s == 2 and ahead2:
                        pe_inproj(pe, g + 2)
                    if s in (3, 4, 5, 6) and ahead1:
                        pe_xgate(pe, g + 1, s - 3)
                    if s == 7 and behind:
                        pe_stats(pe, g - 1)

            def act_z(act, g):
                act.wait_ge(z_ready, g + 1)
                if not isinstance(g, int) or g > 0:
                    act.wait_ge(inp_ready, g)
                for m in range(KI):
                    last = nc.scalar.activation(tz[:, m, :], ps_z[:, m, :], ACT.Tanh, bias=b_in[:, m:m + 1])
                last.then_inc(tz_ready, 1)

            def act_ihi(act, g):
                act.wait_ge(inp_ready, g + 1)
                if after(g):
                    act.wait_ge(xgp_ready, 2 * g)
                nc.scalar.activation(inp_hi[:], inp[:], ACT_ID, scale=w_scale[:, 0, 3:4]).then_inc(ihi_ready, 1)

            def act_xg(act, g, p, half):
                act.wait_ge(xgp_ready, 2 * g + half + 1)
                for m in (2 * half, 2 * half + 1):
                    last = nc.scalar.activation(xg[p][:, :, m, :],
                                                ps_xg[half][:, m % 2, :].rearrange("q (t b) -> q t b", b=B),
                                                ACT_ID, bias=b_g[:, m:m + 1], scale=xg_undo[:, 0:1])
                last.then_inc(xg_ready, 1)

            def act_rows(act, g):
                act.wait_ge(stp_ready, g + 1)
                if not isinstance(g, int) or g > 0:
                    act.wait_ge(rows_moved, 48 * g)
                nc.scalar.copy(rows[:].rearrange("q b t -> q t b"),
                               ps_y[0:96, 0:T * B].rearrange("q (t b) -> q t b", b=B)).then_inc(rows_ready, 1)

            def act_y(act, g):
                act.wait_ge(yp_ready, g + 1)
                if after(g):
                    act.wait_ge(y_ready, g)
                nc.scalar.activation(yb[:], ps_y[:, 0:T * B].rearrange("c (t b) -> c t b", b=B), ACT_ID,
                                     bias=b_out[:, 0:1], scale=w_scale[:, 1, 1:2]).then_inc(yb_ready, 1)

            def act_block(act, g, p, ahead1=True, ahead2=True, behind=True):
                for s in range(T):
                    for half in range(2):
                        act.wait_ge(pre_ready[half], g * T + s + 1)
                        nc.scalar.activation(h_hi[p][:, 2 * half:2 * half + 2, s, :], pre[half][s % 2][:],
                                             ACT.Tanh).then_inc(hi_ready[half], 1)
                        ins = nc.scalar.activation(h[half][:], pre[half][s % 2][:], ACT.Tanh)
                        if half == 0:
                            ins.then_inc(h_ready, 1)
                    act.wait_ge(hi_ready[1], g * T + s + 2)
                    nc.scalar.mul(hi4[1][:], h_hi[p][:, 2:4, s, :], LO_SCALE).then_inc(hi4_ready[1], 1)
                    if s == 1 and behind:
                        act_y(act, g - 1)
                    if s == 2 and ahead2:
                        act_z(act, g + 2)
                    if s == 4 and ahead1:
                        act_xg(act, g + 1, 1 - p, 0)
                    if s == 6 and ahead1:
                        act_xg(act, g + 1, 1 - p, 1)
                    if s == 7 and behind:
                        act_rows(act, g - 1)
                    if s == 7 and ahead2:
                        act_ihi(act, g + 2)

            def dve_inp(dve, g, m):
                if m == 0:
                    dve.wait_ge(tz_ready, g + 1)
                ins = nc.vector.scalar_tensor_tensor(inp[:, m, :], ps_z[:, m, :], b_in[:, m:m + 1], tz[:, m, :],
                                                     ALU.add, ALU.subtract)
                if m == KI - 1:
                    ins.then_inc(inp_ready, 1)

            def dve_ilo(dve, g, m):
                if m == 0:
                    dve.wait_ge(ihi_ready, g + 1)
                ins = nc.vector.scalar_tensor_tensor(inp_lo[:, m, :], inp[:, m, :], w_scale[:, 0, 3:4],
                                                     inp_hi[:, m, :], ALU.mult, ALU.subtract)
                if m == KI - 1:
                    ins.then_inc(ilo_ready, 1)

            def dve_guard(dve, g):
                dve.wait_ge(var_ready, g + 1)
                nc.vector.tensor_scalar(ln_t[:, 2, :], ln_t[:, 1, :], 0.0, 1e-5, ALU.max, ALU.add
                                        ).then_inc(sm_ready, 1)

            def dve_decay(dve, g, p, s):
                if s == 0:
                    dve.wait_ge(cur_ready, g + 1)
                if s or after(g):
                    dve.wait_ge(mem_ready, g * (T + 1) + s)
                nc.vector.scalar_tensor_tensor(memp[:, s:s + 1], mem[:], DECAY, cur[p][:, s:s + 1], ALU.mult, ALU.add
                                               ).then_inc(memp_ready, 1)

            def dve_reset(dve, g, s):
                dve.wait_ge(memp_ready, g * T + s + 1)
                nc.vector.scalar_tensor_tensor(mem[:], memp[:, s:s + 1], 1.0, memp[:, s:s + 1],
                                               ALU.is_lt, ALU.mult).then_inc(mem_ready, 1)
                if s == T - 1:
                    nc.vector.tensor_scalar(spikes[:, bass.ds(g * T, T)], memp[:], 1.0, None, ALU.is_ge
                                            ).then_inc(mem_ready, 1)

            def dve_block(dve, g, p, ahead1=True, ahead2=True, behind2=True, behind3=True):
                if not after(g):
                    dve.wait_ge(xg_ready, 2)
                for s in range(T):
                    for half in range(2):
                        dve.wait_ge(psum_ready[half], g * T + s + 1)
                        nc.vector.scalar_tensor_tensor(
                            pre[half][s % 2][:].rearrange("q m b -> q (m b)"), ps_h[half][s % 2][:, 0:2 * B],
                            w_scale[:, 1, 0:1], xg[p][:, s, 2 * half:2 * half + 2, :].rearrange("q m b -> q (m b)"),
                            ALU.mult, ALU.add).then_inc(pre_ready[half], 1)
                    dve.wait_ge(h_ready, g * T + s + 1)
                    nc.vector.tensor_scalar(hi4[0][:], h_hi[p][:, 0:2, s, :], LO_SCALE, None, ALU.mult
                                            ).then_inc(hi4_ready[0], 1)
                    for half in range(2):
                        dve.wait_ge(hi4_ready[half], g * T + s + 1)
                        nc.vector.scalar_tensor_tensor(h_lo[p][:, 2 * half:2 * half + 2, s, :], h[half][:], LO_SCALE,
                                                       hi4[half][:], ALU.mult, ALU.subtract
                                                       ).then_inc(lo_ready[half], 1)
                    if behind3:
                        dve_decay(dve, g - 3, 1 - p, s)
                    if s in (0, 1) and ahead1:
                        dve_ilo(dve, g + 1, s)
                    if s in (3, 4) and ahead2:
                        dve_inp(dve, g + 2, s - 3)
                    if s == 5 and behind2:
                        dve_guard(dve, g - 2)
                    if behind3:
                        dve_reset(dve, g - 3, s)

            def pool_xn(pool, g):
                if not isinstance(g, int) or g > 0:
                    pool.wait_ge(z_ready, g)
                nc.gpsimd.tensor_tensor(xn_s[:], tokens(g), scale_cb[:].unsqueeze(1).to_broadcast([C, T, B]),
                                        ALU.mult).then_inc(xn_step, 1)
                pool.wait_ge(xn_step, g + 1)
                nc.gpsimd.tensor_tensor(xn[:], xn_s[:], shift_cb[:].unsqueeze(1).to_broadcast([C, T, B]),
                                        ALU.add).then_inc(xn_ready, 1)

            def pool_y(pool, g):
                pool.wait_ge(yb_ready, g + 1)
                if after(g):
                    pool.wait_ge(stp_ready, g)
                nc.gpsimd.tensor_tensor(y[:], yb[:], tokens(g), ALU.add).then_inc(y_ready, 1)
                pool.wait_ge(y_ready, g + 1)
                nc.gpsimd.tensor_tensor(ysq[:], y[:], y[:], ALU.mult).then_inc(ysq_ready, 1)
                nc.gpsimd.tensor_copy(tokens(g), y[:])

            def pool_var(pool, g):
                pool.wait_ge(rows_moved, 48 * g + 48)
                if after(g):
                    pool.wait_ge(cur_ready, g)
                mean, square = sm[:, 0, :], sm[:, 2, :]
                ch = Chain(pool, ln_step, g * 3)
                ch.step(nc.gpsimd.tensor_tensor(ln_t[:, 0, :], mean, mean, ALU.mult))
                nc.gpsimd.tensor_tensor(ln_t[:, 1, :], square, ln_t[:, 0, :], ALU.subtract).then_inc(var_ready, 1)

            def pool_ln(pool, g, p, free=True):
                pool.wait_ge(sm_ready, g + 1)
                mean, dot = sm[:, 0, :], sm[:, 1, :]
                r = ln_t[:, 3, :]
                ch = Chain(pool, ln_step, g * 3 + 1)
                ch.step(nc.gpsimd.tensor_tensor(r, ln_t[:, 2, :], half_neg[:], ALU.pow))
                nc.gpsimd.tensor_tensor(ln_r[:, bass.ds(g * T, T)], r, one8[:], ALU.mult)
                nc.gpsimd.tensor_tensor(ln_mr[:, bass.ds(g * T, T)], mean, r, ALU.mult)
                ch.step(nc.gpsimd.tensor_tensor(ln_t[:, 4, :], dot, r, ALU.mult))
                if free:
                    pool.wait_ge(mem_ready, (g - 1) * (T + 1))
                nc.gpsimd.tensor_tensor(cur[p][:], ln_t[:, 4, :], bs[:, 0:1].to_broadcast([B, T]), ALU.add
                                        ).then_inc(cur_ready, 1)

            def pool_block(pool, g, p, ahead3=True, behind=True, behind2=True, behind3=True):
                if behind:
                    pool_y(pool, g - 1)
                if behind2:
                    pool_var(pool, g - 2)
                if ahead3:
                    pool_xn(pool, g + 3)
                if behind2:
                    pool_ln(pool, g - 2, p, behind3)

            FRONT, TAIL = 4, 4

            def run(eng, one):
                for g in range(FRONT):
                    one(eng, g, g % 2)
                with eng.Fori(0, (NBLK - FRONT - TAIL) // 2) as it:
                    for q in range(2):
                        one(eng, it * 2 + (FRONT + q), q)
                for g in range(NBLK - TAIL, NBLK):
                    one(eng, g, g % 2)

            def near(g, lo=0, hi=NBLK):
                return not isinstance(g, int) or lo <= g < hi

            @block.tensor
            def _(pe):
                pe.wait_ge(loaded, 16 * NLOADS)
                nc.tensor.matmul(ps_y[:, 0:1], mean_w[:], ws[:]).then_inc(mean_ready, 1)
                pe.wait_ge(bound_step, 2)
                for m in range(KI):
                    last = nc.tensor.matmul(ps_z[:, m, 0:1], inp[:, 0, m * 128:(m + 1) * 128], xn_max[:],
                                            start=(m == 0), stop=True, skip_group_check=True)
                last.then_inc(mean_ready, 1)
                pe.wait_ge(setup, SETUP)
                pe_inproj(pe, 0)
                for m in range(KH):
                    pe_xgate(pe, 0, m)
                pe_inproj(pe, 1)
                run(pe, lambda e, g, p: pe_block(e, g, p, near(g + 1), near(g + 2), near(g - 1)))
                for half in range(2):
                    pe.wait_ge(lo_ready[half], L + 1)
                pe_yproj(pe, NBLK - 1, 1, 0)
                pe_yproj(pe, NBLK - 1, 1, 1)
                pe_stats(pe, NBLK - 1)

            @block.scalar
            def _(act):
                for dst, name in ((w_in[:], "L0_conv_w_in"), (b_in[:], "L0_conv_b_in"), (gb[:, 0:1], "L0_conv_gamma"),
                                  (gb[:, 1:2], "L0_conv_beta"), (ws[:], "L1_attn_Ws"), (b_ih[:], "L0_conv_b_ih"),
                                  (b_hh[:], "L0_conv_b_hh"), (b_out[:], "L0_conv_b_out")):
                    act.dma_start(dst, d[name]).then_inc(loaded, 16)
                act.dma_start(bs[:], d["L1_attn_bs"].partition_broadcast(B)).then_inc(loaded, 16)
                for n, hi, hi_s in ((HI_STEP, w_hi, w_hi_s), (HI_STEP + 1, o_hi, o_hi_s)):
                    act.wait_ge(w_step, n)
                    nc.scalar.mul(hi_s[:], hi[:], 1.0 / LO_SCALE).then_inc(setup, 1)
                act.wait_ge(loaded, 16 * NLOADS)
                act.wait_ge(setup, SETUP)
                act_z(act, 0)
                act_ihi(act, 0)
                act_z(act, 1)
                act_xg(act, 0, 0, 0)
                act_xg(act, 0, 0, 1)
                act_ihi(act, 1)
                run(act, lambda e, g, p: act_block(e, g, p, near(g + 1), near(g + 2), near(g - 1)))
                act_y(act, NBLK - 1)
                act_rows(act, NBLK - 1)

            @block.vector
            def _(dve):
                v = nc.vector
                dve.wait_ge(loaded, 16 * NLOADS)
                bch = Chain(dve, bound_step)
                v.scalar_tensor_tensor(inp[:, 0, :], w_in[:], -1.0, w_in[:], ALU.mult, ALU.max)
                bch.step(v.scalar_tensor_tensor(gb_abs[:], gb[:], -1.0, gb[:], ALU.mult, ALU.max))
                bch.step(v.scalar_tensor_tensor(xn_max[:], gb_abs[:, 0:1], BN_MAX, gb_abs[:, 1:2], ALU.mult, ALU.add))
                bch.step(v.scalar_tensor_tensor(b_abs[:], b_in[:], -1.0, b_in[:], ALU.mult, ALU.max))
                for i, w in enumerate((w_hh, w_out, w_ih)):
                    v.tensor_reduce(w_abs[:, 0, i:i + 1], w.rearrange("p k m -> p (k m)"), AX_X, ALU.max,
                                    apply_absolute_value=True)
                dve.wait_ge(mean_ready, 2)
                bch.step(v.tensor_tensor(z_max[:], ps_z[:, :, 0], b_abs[:], ALU.add))
                v.tensor_reduce(w_abs[:, 0, 3:4], z_max[:], AX_X, ALU.max).then_inc(w_max, 1)
                v.memset(mem[:], 0.0).then_inc(setup, 1)
                v.memset(half_neg[:], -0.5).then_inc(setup, 1)
                v.memset(one8[:], 1.0).then_inc(setup, 1)
                v.tensor_tensor(b_g[:], b_ih[:], b_hh[:], ALU.add).then_inc(setup, 1)
                for half in range(2):
                    ks = slice(2 * half, 2 * half + 2)
                    v.memset(h_hi[1][:, ks, T - 1, :], 0.0).then_inc(hi_ready[half], 1)
                    v.memset(h_lo[1][:, ks, T - 1, :], 0.0).then_inc(lo_ready[half], 1)
                dve.wait_ge(w_max, 2)
                ch = Chain(dve, w_step)
                ch.step(v.tensor_scalar(w_abs[:, 3, :], w_abs[:, 1, :], 1e-30, None, ALU.max))
                ch.step(v.tensor_scalar(w_abs[:, 2, :].bitcast(I32), w_abs[:, 3, :].bitcast(I32), 0x7F800000, None,
                                        ALU.bitwise_and))
                ch.step(v.reciprocal(w_abs[:, 3, :], w_abs[:, 2, :]))
                ch.step(v.tensor_scalar(w_scale[:, 0, :], w_abs[:, 3, :], W_TOP, None, ALU.mult))
                ch.step(v.tensor_scalar(w_scale[:, 1, :], w_abs[:, 2, :], 1.0 / W_TOP, None, ALU.mult))
                v.tensor_tensor(xg_undo[:], w_scale[:, 1, 2:3], w_scale[:, 1, 3:4], ALU.mult).then_inc(setup, 1)
                for i, (w, hi, lo) in enumerate(((w_hh, w_hi, w_lo), (w_out, o_hi, o_lo), (w_ih, i_hi, i_lo))):
                    scale = w_scale[:, 0, i:i + 1]
                    ch.step(v.tensor_scalar(hi[:], w, scale, None, ALU.mult))
                    v.scalar_tensor_tensor(lo[:], w, scale, hi[:], ALU.mult, ALU.subtract).then_inc(setup, 1)
                dve.wait_ge(mean_ready, 1)
                ch.step(v.tensor_tensor(ws_c[:], ws[:], ps_y[:, 0:1], ALU.subtract))
                v.memset(stat_w[:, 0, :], 1.0 / C).then_inc(setup, 1)
                v.tensor_copy(stat_w[:, 1, :], ws_c[:].to_broadcast([C, 32])).then_inc(setup, 1)
                dve.wait_ge(setup, SETUP)
                for m in range(KI):
                    dve_inp(dve, 0, m)
                for m in range(KI):
                    dve_ilo(dve, 0, m)
                dve.wait_ge(ilo_ready, 1)
                for m in range(KI):
                    dve_inp(dve, 1, m)
                run(dve, lambda e, g, p: dve_block(e, g, p, near(g + 1), near(g + 2), near(g - 2), near(g - 3)))
                for g in (NBLK - 3, NBLK - 2, NBLK - 1):
                    if g > NBLK - 3:
                        dve_guard(dve, g)
                    for s in range(T):
                        dve_decay(dve, g, g % 2, s)
                        dve_reset(dve, g, s)

            @block.gpsimd
            def _(pool):
                pool.wait_ge(w_max, 1)
                nc.gpsimd.partition_all_reduce(w_abs[:, 1, :], w_abs[:, 0, :], 128, bass.bass_isa.ReduceOp.max
                                               ).then_inc(w_max, 1)
                pool.wait_ge(setup, SETUP)
                pool.wait_ge(loaded, 16 * NLOADS)
                for g in range(3):
                    pool_xn(pool, g)
                run(pool, lambda e, g, p: pool_block(e, g, p, near(g + 3), near(g - 1), near(g - 2), near(g - 3)))
                pool_y(pool, NBLK - 1)
                for g in (NBLK - 2, NBLK - 1):
                    pool_var(pool, g)
                    pool_ln(pool, g, g % 2)


def after(g, n=1):
    return not isinstance(g, int) or g >= n


def apart(eng, sem):
    eng.sem_inc(sem, 1)


def pipelined(eng, count, front, tail, one):
    for i in range(front):
        one(i, i // 2, i % 2)
    with eng.Fori(0, (count - front - tail) // 2) as it:
        for p in range(2):
            one(it * 2 + (front + p), it + front // 2, p)
    for i in range(count - tail, count):
        one(i, i // 2, i % 2)


def build_mask(nc, d, spikes, ln_r, ln_mr, mask, wvo, bvo):
    with ExitStack() as ctx:
        st = Store(nc, ctx)
        ones = st.sb("ones", [B, Q])
        key_bias = st.sb("key_bias", [Q, L])
        local_bias = st.sb("local_bias", [Q, L])
        tri = st.sb("tri", [Q, 2 * Q])
        wv_t = st.sb("wv_t", [C, C])
        wo = st.sb("wo", [C, C])
        bv = st.sb("bv", [C, 1])
        bv_cols = st.sb("bv_cols", [C, C])
        ps_n = st.ps("ps_n", [Q, 2, 512])
        ps_w = st.ps("ps_w", [C, 2, 512])
        loaded = st.sem("mask_loaded")
        ready = st.sem("mask_inputs_ready")
        counted = st.sem("counted")
        step = st.sem("mask_step")
        saved = st.sem("ln_saved")

        with nc.Block() as block:
            @block.sync
            def _(sp):
                sp.dma_start(d["s_ln"][0], ln_r[:]).then_inc(saved, 16)
                sp.dma_start(d["s_ln"][1], ln_mr[:]).then_inc(saved, 16)
                sp.wait_ge(saved, 32)

            @block.scalar
            def _(act):
                for dst, name in ((tri, "c_tri"), (wv_t, "L1_attn_Wv"), (wo, "L1_attn_Wo"), (bv, "L1_attn_bv")):
                    act.dma_start(dst[:], d[name]).then_inc(loaded, 16)

            @block.tensor
            def _(pe):
                pe.wait_ge(ready, 1)
                for h in range(2):
                    last = nc.tensor.matmul(ps_n[:, h, :], ones[:], spikes[:, h * 512:(h + 1) * 512])
                last.then_inc(counted, 1)
                pe.wait_ge(loaded, 64)
                nc.tensor.matmul(ps_w[:, 0, 0:C], wv_t[:], wo[:])
                pe.wait_ge(ready, 2)
                nc.tensor.matmul(ps_w[:, 1, 0:C], bv_cols[:], wo[:]).then_inc(counted, 1)

            @block.vector
            def _(dve):
                v = nc.vector
                v.memset(ones[:], 1.0).then_inc(ready, 1)
                dve.wait_ge(loaded, 64)
                v.tensor_copy(bv_cols[:], bv[:, 0:1].to_broadcast([C, C])).then_inc(ready, 1)
                dve.wait_ge(counted, 1)
                ch = Chain(dve, step)
                ch.step(v.tensor_scalar(key_bias[:], ps_n[:].rearrange("p a b -> p (a b)"), 0.5, NEG,
                                        ALU.is_lt, ALU.mult))
                ch.step(v.tensor_copy(local_bias[:], key_bias[:]))
                ch.step(v.memset(local_bias[:].rearrange("p (a b) -> p a b", b=STRIDE)[:, :, 0], NEG))
                ch.step(v.memset(local_bias[:, 0:FIRST], NEG))
                for i in range(NQ):
                    lo = 0 if i else Q
                    v.tensor_tensor(mask[:, i, lo:2 * Q], tri[:, lo:2 * Q],
                                    local_bias[:, (i - 1) * Q + lo:(i + 1) * Q], ALU.add)
                    v.tensor_copy(mask[:, i, 2 * Q:2 * Q + FIRST], key_bias[:, 0:FIRST])
                    v.tensor_copy(mask[:, i, 2 * Q + FIRST:],
                                  key_bias[:].rearrange("p (a b) -> p a b", b=STRIDE)[:, 1:, 0])
                dve.wait_ge(counted, 2)
                v.tensor_copy(wvo[:], ps_w[:, 0, 0:C])
                v.tensor_copy(bvo[:], ps_w[:, 1, 0:C])


def attention(nc, d, x_sb, mask, wvo, bvo):
    NK = 2 * Q + NG
    LAG_T, LAG_V = 2, 3
    with ExitStack() as ctx:
        st = Store(nc, ctx)
        wq, wk = st.sb("wq", [C, C]), st.sb("wk", [C, C])
        bq, bk, bo = st.sb("bq", [C, 1]), st.sb("bk", [C, 1]), st.sb("bo", [C, 1])
        ident = st.sb("ident", [128, 128])
        r_b, mr_b = st.sb("r_b", [C, L]), st.sb("mr_b", [C, L])
        xr = st.sb("xr", [C, L])
        ln = st.sb("ln", [C, L])
        ln_g = st.sb("ln_g", [C, NG])
        qt = [st.sb(f"qt{p}", [C, L]) for p in range(2)]
        kt = [st.sb(f"kt{p}", [C, NQ, NK]) for p in range(2)]
        vt = [st.sb(f"vt{p}", [Q, NQ, C]) for p in range(2)]
        vg = [st.sb(f"vg{p}", [NG, C]) for p in range(2)]
        pr = [st.sb(f"pr{i}", [Q, NK]) for i in range(4)]
        pt = [st.sb(f"pt{i}", [Q, 3, Q]) for i in range(2)]
        mx, nm, den, rden, rv = (st.sb(n, [Q, 2 * NQ]) for n in ("mx", "nm", "den", "rden", "rv"))
        ps_p = [st.ps(f"ps_p{i}", [128, 512]) for i in range(2)]
        ps_s = [st.ps(f"ps_s{i}", [128, 512]) for i in range(2)]
        ps_t = [st.ps(f"ps_t{i}", [128, 4, Q]) for i in range(2)]
        ps_o = [st.ps(f"ps_o{i}", [128, 512]) for i in range(2)]

        loaded = st.sem("attn_loaded")
        waits_apart = st.sem("attn_waits_apart")
        bc_loaded = st.sem("ln_factors_loaded")
        xr_ready = st.sem("xr_ready")
        ln_ready = st.sem("ln_ready")
        lng_ready = st.sem("lng_ready")
        proj_done = st.sem("proj_done")
        qk_evac = st.sem("qk_evac")
        v_evac = st.sem("v_evac")
        kt_ready = st.sem("kt_ready")
        before_ready = st.sem("keys_before_ready")
        s_done = st.sem("s_done")
        masked = st.sem("masked")
        nm_ready = st.sem("nm_ready")
        exp_done = st.sem("exp_done")
        norm_step = st.sem("norm_step")
        p_ready = st.sem("p_ready")
        t_done = st.sem("t_done")
        pt_ready = st.sem("pt_ready")
        pv_done = st.sem("pv_done")
        o_added = st.sem("o_added")

        def back(b, p, i, lag):
            return (b, p, i - lag) if i >= lag else (b - 1, 1 - p, i - lag + NQ)

        def xb(b):
            return x_sb[:, bass.ds(b, 1), :].rearrange("c b l -> c (b l)")

        with nc.Block() as block:
            @block.sync
            def _(sp):
                def factors(b):
                    if after(b):
                        sp.wait_ge(ln_ready, b)
                    for i, dst in enumerate((r_b, mr_b)):
                        sp.dma_start(dst[:], d["s_ln"][i, bass.ds(b, 1), :].rearrange("b l -> (b l)")
                                     .partition_broadcast(C)).then_inc(bc_loaded, 16)

                factors(0)
                with sp.Fori(1, B) as b:
                    factors(b)
                sp.wait_ge(bc_loaded, 32 * B)

            def pe_proj(pe, b, p, piece):
                kind, h = (("q", 0), ("q", 1), ("k", 0), ("k", 1), ("v", 0), ("v", 1), ("g", 0))[piece]
                bank = ps_p[h]
                if piece == 0:
                    pe.wait_ge(ln_ready, b + 1)
                    if after(b):
                        pe.wait_ge(v_evac, 3 * b)
                if piece in (2, 3, 4, 5):
                    pe.wait_ge(qk_evac, 4 * b + piece - 1)
                if kind in "qk":
                    last = nc.tensor.matmul(bank[:], (wq if kind == "q" else wk)[:], ln[:, h * 512:(h + 1) * 512])
                elif kind == "v":
                    for i in range(4):
                        j = 4 * h + i
                        last = nc.tensor.matmul(bank[:, i * C:(i + 1) * C], ln[:, j * Q:(j + 1) * Q], wvo[:],
                                                start=(i == 0), stop=True, skip_group_check=True)
                else:
                    pe.wait_ge(lng_ready, b + 1)
                    pe.wait_ge(v_evac, 3 * b + 1)
                    last = nc.tensor.matmul(bank[0:NG, 0:C], ln_g[:], wvo[:])
                last.then_inc(proj_done, 1)

            def pe_scores(pe, b, p, i):
                n = b * NQ + i
                if i == 0:
                    pe.wait_ge(kt_ready, b + 1)
                    pe.wait_ge(before_ready, 2 * b + 2)
                if after(n, 2):
                    pe.wait_ge(masked, n - 1)
                lo = 0 if i else Q
                nc.tensor.matmul(ps_s[i % 2][:, lo:NK], qt[p][:, i * Q:(i + 1) * Q], kt[p][:, i, lo:NK]
                                 ).then_inc(s_done, 1)

            def pe_transpose(pe, b, p, i):
                n = b * NQ + i
                pe.wait_ge(p_ready, n + 1)
                if after(n, 2):
                    pe.wait_ge(pt_ready, n - 1)
                w = pr[i % 4]
                out = ps_t[i % 2]
                if i:
                    nc.tensor.transpose(out[:, 0, :], w[:, 0:Q], ident[:])
                nc.tensor.transpose(out[:, 1, :], w[:, Q:2 * Q], ident[:])
                nc.tensor.transpose(out[0:NG, 2, :], w[:, 2 * Q:NK], ident[:]).then_inc(t_done, 1)

            def pe_values(pe, b, p, i):
                n = b * NQ + i
                pe.wait_ge(pt_ready, n + 1)
                if i == 0:
                    pe.wait_ge(v_evac, 3 * b + 3)
                if i % 4 == 0 and after(b):
                    pe.wait_ge(o_added, 2 * b + i // 4 - 1)
                out = ps_o[i // 4][:, (i % 4) * Q:(i % 4 + 1) * Q]
                w = pt[i % 2]
                if i:
                    nc.tensor.matmul(out, vt[p][:, i - 1, :], w[:, 0, :], start=(i % 4 == 0), stop=False,
                                     skip_group_check=True)
                nc.tensor.matmul(out, vt[p][:, i, :], w[:, 1, :], start=(i == 0), stop=False, skip_group_check=True)
                nc.tensor.matmul(out, vg[p][:], w[0:NG, 2, :], start=False, stop=True, skip_group_check=True
                                 ).then_inc(pv_done, 1)

            @block.tensor
            def _(pe):
                pe.wait_ge(loaded, 96)
                for piece in range(7):
                    pe_proj(pe, 0, 0, piece)

                def one(b, half, p):
                    for i in range(NQ):
                        pe_scores(pe, b, p, i)
                        if i >= LAG_T or after(b):
                            pe_transpose(pe, *back(b, p, i, LAG_T))
                        if i >= LAG_V or after(b):
                            pe_values(pe, *back(b, p, i, LAG_V))
                        if i >= 2 and not (isinstance(b, int) and b == B - 1):
                            pe_proj(pe, b + 1, 1 - p, i - 2)
                            if i == NQ - 1:
                                pe_proj(pe, b + 1, 1 - p, 6)

                pipelined(pe, B, 2, 2, one)
                for i in range(LAG_V):
                    if i < LAG_T:
                        pe_transpose(pe, B - 1, 1, NQ - LAG_T + i)
                    pe_values(pe, B - 1, 1, NQ - LAG_V + i)

            def act_proj(act, b, p, piece):
                act.wait_ge(proj_done, 7 * b + piece + 1)
                h = piece % 2
                if piece < 2:
                    nc.scalar.activation(qt[p][:, h * 512:(h + 1) * 512], ps_p[h][:], ACT_ID, bias=bq[:, 0:1]
                                         ).then_inc(qk_evac, 1)
                else:
                    nc.scalar.activation(kt[p][:, 4 * h:4 * h + 4, Q:2 * Q],
                                         ps_p[h][:].rearrange("c (i q) -> c i q", q=Q), ACT_ID, bias=bk[:, 0:1]
                                         ).then_inc(qk_evac, 1)

            def act_exp(act, b, p, i):
                n = b * NQ + i
                lo, c = (0 if i else Q), NQ * p + i
                act.wait_ge(nm_ready, n + 1)
                nc.scalar.activation(pr[i % 4][:, lo:NK], pr[i % 4][:, lo:NK], ACT.Exp, bias=nm[:, c:c + 1],
                                     scale=SCALE, accum_out=den[:, c:c + 1]).then_inc(exp_done, 1)

            def act_pt(act, b, p, i):
                n = b * NQ + i
                act.wait_ge(t_done, n + 1)
                if after(n, 2):
                    act.wait_ge(pv_done, n - 1)
                lo = 0 if i else 1
                nc.scalar.copy(pt[i % 2][:, lo:2, :], ps_t[i % 2][:, lo:2, :])
                nc.scalar.copy(pt[i % 2][0:NG, 2, :], ps_t[i % 2][0:NG, 2, :]).then_inc(pt_ready, 1)

            @block.scalar
            def _(act):
                for dst, name in ((wq, "L1_attn_Wq"), (wk, "L1_attn_Wk"), (bq, "L1_attn_bq"), (bk, "L1_attn_bk"),
                                  (bo, "L1_attn_bo"), (ident, "c_ident")):
                    act.dma_start(dst[:], d[name]).then_inc(loaded, 16)
                act.wait_ge(loaded, 96)
                for piece in range(4):
                    act_proj(act, 0, 0, piece)

                def one(b, half, p):
                    for i in range(NQ):
                        if i >= LAG_T or after(b):
                            act_pt(act, *back(b, p, i, LAG_T))
                        act_exp(act, b, p, i)
                        if 2 <= i < 6 and not (isinstance(b, int) and b == B - 1):
                            act_proj(act, b + 1, 1 - p, i - 2)

                pipelined(act, B, 2, 2, one)
                for i in range(NQ - LAG_T, NQ):
                    act_pt(act, B - 1, 1, i)

            def dve_before(dve, b, p, h):
                dve.wait_ge(qk_evac, 4 * b + 3 + h)
                apart(dve, waits_apart)
                n = min(4, NQ - 1 - 4 * h)
                nc.vector.tensor_copy(kt[p][:, 4 * h + 1:4 * h + 1 + n, 0:Q], kt[p][:, 4 * h:4 * h + n, Q:2 * Q]
                                      ).then_inc(before_ready, 1)

            def dve_values(dve, b, p, piece):
                dve.wait_ge(proj_done, 7 * b + 5 + piece)
                if piece < 2:
                    nc.vector.tensor_tensor(vt[p][:, 4 * piece:4 * piece + 4, :],
                                            ps_p[piece][:].rearrange("q (i c) -> q i c", c=C),
                                            bvo[:].unsqueeze(1).to_broadcast([Q, 4, C]), ALU.add
                                            ).then_inc(v_evac, 1)
                else:
                    nc.vector.tensor_tensor(vg[p][:], ps_p[0][0:NG, 0:C], bvo[0:NG, :], ALU.add).then_inc(v_evac, 1)

            def dve_mask(dve, b, p, i):
                n = b * NQ + i
                lo, c = (0 if i else Q), NQ * p + i
                dve.wait_ge(s_done, n + 1)
                if after(n, 4):
                    dve.wait_ge(t_done, n - 3)
                apart(dve, waits_apart)
                nc.vector.tensor_tensor_reduce(pr[i % 4][:, lo:NK], ps_s[i % 2][:, lo:NK], mask[:, i, lo:NK], 1.0,
                                               -3.0e38, ALU.add, ALU.max, mx[:, c:c + 1]).then_inc(masked, 1)
                dve.wait_ge(masked, n + 1)
                nc.vector.tensor_scalar(nm[:, c:c + 1], mx[:, c:c + 1], -SCALE, None, ALU.mult).then_inc(nm_ready, 1)

            def dve_norm(dve, b, p, i):
                n = b * NQ + i
                lo, c = (0 if i else Q), NQ * p + i
                dve.wait_ge(exp_done, n + 1)
                ch = Chain(dve, norm_step, n * 2)
                ch.step(nc.vector.reciprocal(rden[:, c:c + 1], den[:, c:c + 1]))
                ch.step(nc.vector.scalar_tensor_tensor(rv[:, c:c + 1], mx[:, c:c + 1], NEG / 2, rden[:, c:c + 1],
                                                       ALU.is_gt, ALU.mult))
                nc.vector.tensor_scalar(pr[i % 4][:, lo:NK], pr[i % 4][:, lo:NK], rv[:, c:c + 1], None, ALU.mult
                                        ).then_inc(p_ready, 1)

            def dve_out(dve, b, h):
                dve.wait_ge(pv_done, b * NQ + 4 * h + 4)
                xs = xb(b)[:, h * 512:(h + 1) * 512]
                nc.vector.scalar_tensor_tensor(xs, ps_o[h][:], bo[:, 0:1], xs, ALU.add, ALU.add).then_inc(o_added, 1)

            @block.vector
            def _(dve):
                dve.wait_ge(loaded, 96)
                for h in range(2):
                    dve_before(dve, 0, 0, h)
                for piece in range(3):
                    dve_values(dve, 0, 0, piece)

                def one(b, half, p):
                    more = not (isinstance(b, int) and b == B - 1)
                    for i in range(NQ):
                        dve_mask(dve, b, p, i)
                        if i >= 1 or after(b):
                            dve_norm(dve, *back(b, p, i, 1))
                        if i == 1 and after(b):
                            for piece in (1, 2):
                                dve_values(dve, b, p, piece)
                        if i in (5, 6) and more:
                            dve_before(dve, b + 1, 1 - p, i - 5)
                        if i == 7 and more:
                            dve_values(dve, b + 1, 1 - p, 0)
                        if i == 3 and after(b):
                            dve_out(dve, b - 1, 1)
                        if i == 7:
                            dve_out(dve, b, 0)

                pipelined(dve, B, 2, 2, one)
                dve_norm(dve, B - 1, 1, NQ - 1)
                dve_out(dve, B - 1, 1)

            @block.gpsimd
            def _(pool):
                def scale(b):
                    pool.wait_ge(bc_loaded, 32 * b + 32)
                    nc.gpsimd.tensor_tensor(xr[:], xb(b), r_b[:], ALU.mult).then_inc(xr_ready, 1)

                def centre(b):
                    pool.wait_ge(xr_ready, b + 1)
                    if after(b):
                        pool.wait_ge(proj_done, 7 * b)
                    nc.gpsimd.tensor_tensor(ln[:], xr[:], mr_b[:], ALU.subtract).then_inc(ln_ready, 1)
                    pool.wait_ge(ln_ready, b + 1)
                    apart(pool, waits_apart)
                    by_stride = ln[:].rearrange("c (a s) -> c a s", s=STRIDE)
                    nc.gpsimd.tensor_copy(ln_g[:, 0:FIRST], ln[:, 0:FIRST])
                    nc.gpsimd.tensor_copy(ln_g[:, FIRST:], by_stride[:, 1:, 0]).then_inc(lng_ready, 1)

                def keys(b, p):
                    pool.wait_ge(qk_evac, 4 * b + 4)
                    apart(pool, waits_apart)
                    k = kt[p]
                    g0 = 2 * Q + FIRST
                    nc.gpsimd.tensor_copy(k[:, :, 2 * Q:g0], k[:, 0:1, Q:Q + FIRST].to_broadcast([C, NQ, FIRST]))
                    nc.gpsimd.tensor_copy(k[:, :, g0:NK:2], k[:, :, Q + STRIDE].unsqueeze(1).to_broadcast([C, NQ, NQ]))
                    nc.gpsimd.tensor_copy(k[:, :, g0 + 1:NK:2],
                                          k[:, 1:NQ, Q].unsqueeze(1).to_broadcast([C, NQ, NQ - 1])
                                          ).then_inc(kt_ready, 1)

                scale(0)
                centre(0)
                keys(0, 0)
                scale(1)

                def one(b, half, p):
                    if not (isinstance(b, int) and b == B - 1):
                        centre(b + 1)
                        if not (isinstance(b, int) and b == B - 2):
                            scale(b + 2)
                        keys(b + 1, 1 - p)

                pipelined(pool, B, 2, 2, one)


def route(nc, d, x_sb, pooled):
    NP = B // 2
    GONE = -3.0e38
    with ExitStack() as ctx:
        st = Store(nc, ctx)
        ident = st.sb("ident_r", [128, 128])
        gate_w = st.sb("gate_w", [C, E])
        gate_b = st.sb("gate_b", [2 * E, 1])
        xs = [st.sb(f"xs{p}", [C, L]) for p in range(2)]
        half_neg = st.sb("half_neg_r", [Q, NQ])
        bn = st.sb("bn_r", [Q, NQ, 6])
        mv = st.sb("mv_r", [Q, NQ, 2])
        ve = st.sb("ve", [Q, NQ])
        rs = st.sb("rs", [Q, NQ])
        raw = [st.sb(f"raw{p}", [Q, NQ, C]) for p in range(2)]
        ln = [st.sb(f"ln_tok{i}", [Q, NQ, C]) for i in range(4)]
        ln_t = st.sb("ln_ch", [C, L])
        lg = st.sb("lg", [2 * E, L])
        ex = st.sb("ex", [2 * E, L])
        wt = st.sb("wt", [2 * E, L])
        wn = [st.sb(f"wn{i}", [2 * E, L]) for i in range(2)]
        wn_t = st.sb("wn_t", [Q, NQ, 2 * E])
        top = st.sb("top", [2 * E, TOPK])
        sml = st.sb("sml", [2 * E, 4])
        ps_t = [st.ps(f"ps_rt{i}", [128, 512]) for i in range(2)]
        ps_u = [st.ps(f"ps_ru{i}", [128, 512]) for i in range(2)]
        ps_l = [st.ps(f"ps_rl{i}", [128, 512]) for i in range(2)]
        ps_v = st.ps("ps_rv", [128, 512])
        ps_w = st.ps("ps_rw", [128, 512])

        loaded = st.sem("route_loaded")
        waits_apart = st.sem("route_waits_apart")
        xs_loaded = [st.sem(f"xs_loaded{p}") for p in range(2)]
        t1_done = st.sem("t1_done")
        raw_ready = st.sem("raw_ready")
        bn_done = st.sem("bn_done")
        ve_ready = st.sem("ve_ready")
        rs_ready = st.sem("rs_ready")
        half_ready = st.sem("half_ready")
        ln_ready = st.sem("ln_tok_ready")
        t2_done = st.sem("t2_done")
        lnt_ready = st.sem("ln_ch_ready")
        lg_done = st.sem("lg_done")
        lg_ready = st.sem("lg_ready")
        top_ready = st.sem("top_ready")
        nmx_ready = st.sem("nmx_ready")
        ex_ready = st.sem("ex_ready")
        gone_ready = st.sem("gone_ready")
        wt_ready = st.sem("wt_ready")
        wn_ready = st.sem("wn_ready")
        wn_saved = st.sem("wn_saved")
        t3_done = st.sem("t3_done")
        wnt_ready = st.sem("wnt_ready")
        pool_done = st.sem("pooled_done")
        pooled_read = st.sem("pooled_read")

        def near(b):
            return not isinstance(b, int) or b < B

        with nc.Block() as block:
            @block.sync
            def _(sp):
                for dst, name in ((ident, "c_ident"), (gate_w, "L1_ffn_gate_w"), (gate_b, "L1_ffn_gate_b")):
                    sp.dma_start(dst[:], d[name]).then_inc(loaded, 16)

                def one(b, half, p):
                    if after(b, 2):
                        sp.wait_ge(t1_done, 2 * b - 2)
                    sp.dma_start(xs[p][:], x_sb[:, bass.ds(b, 1), :].rearrange("c b l -> c (b l)")
                                 ).then_inc(xs_loaded[p], 16)

                pipelined(sp, B, 2, 0, one)
                for p in range(2):
                    sp.wait_ge(xs_loaded[p], 16 * NP)

            def pe_t1(pe, b, half, p, h):
                if h == 0:
                    pe.wait_ge(xs_loaded[p], 16 * half + 16)
                if after(b):
                    pe.wait_ge(raw_ready, 2 * b - 1 + h)
                for i in range(4):
                    j = 4 * h + i
                    last = nc.tensor.transpose(ps_t[h][:, i * C:(i + 1) * C], xs[p][:, j * Q:(j + 1) * Q], ident[:])
                last.then_inc(t1_done, 1)

            def pe_t2(pe, b, p4):
                for h in range(2):
                    pe.wait_ge(ln_ready, 2 * b + 1 + h)
                    if after(b):
                        pe.wait_ge(lnt_ready, 2 * b - 1 + h)
                    for i in range(4):
                        last = nc.tensor.transpose(ps_u[h][:, i * Q:(i + 1) * Q], ln[p4][:, 4 * h + i, :], ident[:])
                    last.then_inc(t2_done, 1)

            def pe_logits(pe, b, half, p):
                if p == 0 and after(half):
                    pe.wait_ge(lg_ready, half)
                for h in range(2):
                    pe.wait_ge(lnt_ready, 2 * b + 1 + h)
                    last = nc.tensor.matmul(ps_l[h][E * p:E * p + E, :], gate_w[:], ln_t[:, h * 512:(h + 1) * 512])
                last.then_inc(lg_done, 1)

            def pe_t3(pe, j, jp, h):
                if h == 0:
                    pe.wait_ge(wn_ready, j + 1)
                if h or after(j):
                    pe.wait_ge(wnt_ready, 2 * j + h)
                for i in range(4):
                    k = 4 * h + i
                    last = nc.tensor.transpose(ps_v[:, i * Q:(i + 1) * Q], wn[jp][:, k * Q:(k + 1) * Q], ident[:])
                last.then_inc(t3_done, 1)

            def pe_pool(pe, j, jp):
                pe.wait_ge(wnt_ready, 2 * j + 2)
                if after(j):
                    pe.wait_ge(pooled_read, j)
                for q in range(2):
                    for k in range(NQ):
                        last = nc.tensor.matmul(ps_w[:, q * 128:(q + 1) * 128], ln[2 * jp + q][:, k, :],
                                                wn_t[:, k, :], start=(k == 0 and q == 0), stop=(k == NQ - 1),
                                                skip_group_check=True)
                last.then_inc(pool_done, 1)

            def by_pairs(eng, one):
                pipelined(eng, NP, 2, 2, lambda j, half, jp: one(j, jp))

            @block.tensor
            def _(pe):
                pe.wait_ge(loaded, 48)
                for b in range(2):
                    for h in range(2):
                        pe_t1(pe, b, 0, b, h)

                def one(j, jp):
                    for p in range(2):
                        b = j * 2 + p
                        pe_t2(pe, b, 2 * jp + p)
                        for h in range(2):
                            if p == 1 and after(j):
                                pe_t3(pe, j - 1, 1 - jp, h)
                            if near(b + 2):
                                pe_t1(pe, b + 2, j + 1, p, h)
                        if p == 1 and after(j):
                            pe_pool(pe, j - 1, 1 - jp)
                        pe_logits(pe, b, j, p)

                by_pairs(pe, one)
                for h in range(2):
                    pe_t3(pe, NP - 1, 1, h)
                pe_pool(pe, NP - 1, 1)

            def dve_stats(dve, b, p):
                for h in range(2):
                    dve.wait_ge(raw_ready, 2 * b + 1 + h)
                    for i in range(4 * h, 4 * h + 4):
                        nc.vector.bn_stats(bn[:, i, :], raw[p][:, i, :]).then_inc(bn_done, 1)
                dve.wait_ge(bn_done, b * (2 * NQ) + NQ)
                apart(dve, waits_apart)
                for i in range(NQ):
                    nc.vector.bn_aggr(mv[:, i, :], bn[:, i, :]).then_inc(bn_done, 1)
                dve.wait_ge(bn_done, b * (2 * NQ) + 2 * NQ)
                nc.vector.tensor_scalar(ve[:], mv[:, :, 1], 1e-5, None, ALU.add).then_inc(ve_ready, 1)

            def dve_norm(dve, b, p, p4):
                dve.wait_ge(rs_ready, b + 1)
                for h in range(2):
                    for i in range(4 * h, 4 * h + 4):
                        last = nc.vector.tensor_scalar(ln[p4][:, i, :], raw[p][:, i, :],
                                                       mv[:, i, 0:1], rs[:, i:i + 1], ALU.subtract, ALU.mult)
                    last.then_inc(ln_ready, 1)

            def dve_top(dve, j):
                dve.wait_ge(lg_ready, j + 1)
                apart(dve, waits_apart)
                nc.vector.max(top[:], lg[:]).then_inc(top_ready, 1)
                dve.wait_ge(top_ready, j + 1)
                if after(j):
                    dve.wait_ge(wn_ready, j)
                apart(dve, waits_apart)
                nc.vector.match_replace(wt[:], top[:], lg[:], GONE).then_inc(gone_ready, 1)

            def dve_weights(dve, j):
                dve.wait_ge(ex_ready, j + 1)
                dve.wait_ge(gone_ready, j + 1)
                nc.vector.reciprocal(sml[:, 2:3], sml[:, 1:2]).then_inc(wt_ready, 1)
                nc.vector.scalar_tensor_tensor(wt[:], wt[:], GONE, ex[:], ALU.is_equal, ALU.mult
                                               ).then_inc(wt_ready, 1)

            @block.vector
            def _(dve):
                dve_stats(dve, 0, 0)
                dve_norm(dve, 0, 0, 0)
                dve_stats(dve, 1, 1)

                def one(j, jp):
                    for p in range(2):
                        b = j * 2 + p
                        if p == 0 and after(j):
                            dve_top(dve, j - 1)
                            dve_weights(dve, j - 1)
                        if near(b + 1):
                            if p == 1 and after(j):
                                dve.wait_ge(pool_done, j)
                            dve_norm(dve, b + 1, 1 - p, (2 * jp + p + 1) % 4)
                        if near(b + 2):
                            dve_stats(dve, b + 2, p)

                by_pairs(dve, one)
                dve_top(dve, NP - 1)
                dve_weights(dve, NP - 1)

            def act_raw(act, b, p, h):
                act.wait_ge(t1_done, 2 * b + 1 + h)
                if h == 0 and after(b, 2):
                    act.wait_ge(ln_ready, 2 * b - 2)
                nc.scalar.copy(raw[p][:, 4 * h:4 * h + 4, :], ps_t[h][:].rearrange("q (i c) -> q i c", c=C)
                               ).then_inc(raw_ready, 1)

            def act_lnt(act, b):
                for h in range(2):
                    act.wait_ge(t2_done, 2 * b + 1 + h)
                    if h == 0 and after(b):
                        act.wait_ge(lg_done, b)
                    nc.scalar.copy(ln_t[:, h * 512:(h + 1) * 512], ps_u[h][:]).then_inc(lnt_ready, 1)

            def act_logits(act, j):
                act.wait_ge(lg_done, 2 * j + 2)
                if after(j):
                    act.wait_ge(gone_ready, j)
                nc.scalar.activation(lg[:, 0:512], ps_l[0][:], ACT_ID, bias=gate_b[:, 0:1])
                nc.scalar.activation(lg[:, 512:], ps_l[1][:], ACT_ID, bias=gate_b[:, 0:1]).then_inc(lg_ready, 1)

            def act_exp(act, j):
                act.wait_ge(top_ready, j + 1)
                if after(j):
                    act.wait_ge(wt_ready, 2 * j)
                nc.scalar.mul(sml[:, 0:1], top[:, 0:1], -1.0).then_inc(nmx_ready, 1)
                act.wait_ge(nmx_ready, j + 1)
                nc.scalar.activation(ex[:], lg[:], ACT.Exp, bias=sml[:, 0:1], accum_out=sml[:, 1:2]
                                     ).then_inc(ex_ready, 1)

            def act_weights(act, j, jp):
                act.wait_ge(wt_ready, 2 * j + 2)
                if after(j, 2):
                    act.wait_ge(wn_saved, 16 * j - 16)
                    act.wait_ge(t3_done, 2 * j - 2)
                nc.scalar.mul(wn[jp][:], wt[:], sml[:, 2:3]).then_inc(wn_ready, 1)

            def act_wnt(act, j, h):
                act.wait_ge(t3_done, 2 * j + 1 + h)
                if h == 0 and after(j):
                    act.wait_ge(pool_done, j)
                nc.scalar.copy(wn_t[:, 4 * h:4 * h + 4, :], ps_v[:].rearrange("q (i e) -> q i e", e=2 * E)
                               ).then_inc(wnt_ready, 1)

            def act_pooled(act, j):
                act.wait_ge(pool_done, j + 1)
                for q in range(2):
                    last = nc.scalar.copy(pooled[:, :, bass.ds(j * 2 + q, 1)].rearrange("c e b -> c (e b)"),
                                          ps_w[:, q * (128 + E):q * (128 + E) + E])
                last.then_inc(pooled_read, 1)

            @block.scalar
            def _(act):
                act.wait_ge(loaded, 48)

                for b in range(2):
                    for h in range(2):
                        act_raw(act, b, b, h)

                def one(j, jp):
                    for p in range(2):
                        b = j * 2 + p
                        act_lnt(act, b)
                        if p == 0 and after(j):
                            act_exp(act, j - 1)
                        for h in range(2):
                            if p == 1 and after(j):
                                act_wnt(act, j - 1, h)
                            if near(b + 2):
                                act_raw(act, b + 2, p, h)
                        if p == 0 and after(j):
                            act_weights(act, j - 1, 1 - jp)
                        if p == 1 and after(j):
                            act_pooled(act, j - 1)
                    act_logits(act, j)

                by_pairs(act, one)
                act_exp(act, NP - 1)
                act_weights(act, NP - 1, 1)
                for h in range(2):
                    act_wnt(act, NP - 1, h)
                act_pooled(act, NP - 1)

            @block.gpsimd
            def _(pool):
                nc.gpsimd.memset(half_neg[:], -0.5).then_inc(half_ready, 1)
                pool.wait_ge(half_ready, 1)

                def saved(j, jp):
                    pool.wait_ge(wn_ready, j + 1)
                    if after(j):
                        pool.wait_ge(wn_saved, 16 * j)
                    pool.dma_start(d["s_wn"][bass.ds(j, 1)].rearrange("j e l -> (j e) l"), wn[jp][:]
                                   ).then_inc(wn_saved, 16)

                def rstd(b):
                    pool.wait_ge(ve_ready, b + 1)
                    nc.gpsimd.tensor_tensor(rs[:], ve[:], half_neg[:], ALU.pow).then_inc(rs_ready, 1)

                rstd(0)
                rstd(1)

                def one(j, jp):
                    for p in range(2):
                        b = j * 2 + p
                        if near(b + 2):
                            rstd(b + 2)
                        if p == 0 and after(j):
                            saved(j - 1, 1 - jp)

                by_pairs(pool, one)
                saved(NP - 1, 1)
                pool.wait_ge(wn_saved, 16 * NP)


def experts(nc, d, pooled):
    G = 4
    NGRP = E // G
    with ExitStack() as ctx:
        st = Store(nc, ctx)
        ident = st.sb("ident_e", [128, 128])
        ones = st.sb("ones_e", [1, B])
        w1 = [st.sb(f"w1_{i}", [C, G, H]) for i in range(2)]
        b1 = [st.sb(f"b1_{i}", [1, G, H]) for i in range(2)]
        w2 = [st.sb(f"w2_{i}", [128, G, KE, C]) for i in range(2)]
        b2 = [st.sb(f"b2_{i}", [1, G, C]) for i in range(2)]
        xe = [st.sb(f"xe{i}", [C, G, B]) for i in range(2)]
        he = st.sb("he", [128, H])
        he_t = st.sb("he_t", [128, KE, 128])
        oe = [st.sb(f"oe{i}", [128, C]) for i in range(2)]
        ps_h = [st.ps(f"ps_eh{i}", [128, H]) for i in range(2)]
        ps_t = st.ps("ps_et", [128, KE, 128])
        ps_o = [st.ps(f"ps_eo{i}", [128, 512]) for i in range(2)]
        loaded = st.sem("experts_loaded")
        waits_apart = st.sem("experts_waits_apart")
        ones_ready = st.sem("ones_ready")
        w1_loaded = [st.sem(f"w1_loaded{i}") for i in range(2)]
        w2_loaded = [st.sem(f"w2_loaded{i}") for i in range(2)]
        xe_ready = st.sem("xe_ready")
        h_done = st.sem("eh_done")
        he_ready = st.sem("he_ready")
        t_done = st.sem("et_done")
        het_ready = st.sem("het_ready")
        o_done = st.sem("eo_done")
        oe_ready = st.sem("oe_ready")
        oe_saved = st.sem("oe_saved")

        with nc.Block() as block:
            @block.sync
            def _(sp):
                sp.dma_start(ident[:], d["c_ident"]).then_inc(loaded, 16)

                def one(g, half, p):
                    e = bass.ds(g * G, G)
                    if after(g, 2):
                        sp.wait_ge(h_done, g - 1)
                    sp.dma_start(w1[p][:], d["w1"][e, 0:C, :].rearrange("e c h -> c e h")
                                 ).then_inc(w1_loaded[p], 16)
                    sp.dma_start(b1[p][:], d["w1"][e, C:C + 1, :].rearrange("e c h -> c e h")
                                 ).then_inc(w1_loaded[p], 16)
                    if after(g, 2):
                        sp.wait_ge(o_done, g - 1)
                    sp.dma_start(w2[p][:], d["w2"][e, 0:H, :].rearrange("e (q j) o -> q e (j o)", j=KE)
                                 ).then_inc(w2_loaded[p], 16)
                    sp.dma_start(b2[p][:], d["w2"][e, H:H + 1, :].rearrange("e h o -> h e o")
                                 ).then_inc(w2_loaded[p], 16)

                pipelined(sp, NGRP, 2, 0, one)

            @block.tensor
            def _(pe):
                pe.wait_ge(loaded, 16)
                pe.wait_ge(ones_ready, 1)

                def first(g, half, p):
                    pe.wait_ge(w1_loaded[p], 32 * half + 32)
                    pe.wait_ge(xe_ready, g + 1)
                    if after(g, 2):
                        pe.wait_ge(he_ready, g - 1)
                    for c in range(G):
                        nc.tensor.matmul(ps_h[p][32 * c:32 * c + 32, :], xe[p][:, c, :], w1[p][:, c, :],
                                         start=True, stop=False, skip_group_check=True)
                    for c in range(G):
                        last = nc.tensor.matmul(ps_h[p][32 * c:32 * c + 32, :], ones[:], b1[p][:, c, :],
                                                start=False, stop=True, skip_group_check=True,
                                                tile_position=(0, 32 * c))
                    last.then_inc(h_done, 1)

                def one(g, half, p):
                    pe.wait_ge(he_ready, g + 1)
                    if after(g):
                        pe.wait_ge(het_ready, g)
                    for j in range(KE):
                        last = nc.tensor.transpose(ps_t[:, j, :], he[:].rearrange("q (a j) -> q j a", j=KE)[:, j, :],
                                                   ident[:])
                    last.then_inc(t_done, 1)
                    if not (isinstance(g, int) and g == NGRP - 1):
                        first(g + 1, half + p, 1 - p)
                    pe.wait_ge(w2_loaded[p], 32 * half + 32)
                    pe.wait_ge(het_ready, g + 1)
                    if after(g, 2):
                        pe.wait_ge(oe_ready, g - 1)
                    for j in range(KE):
                        for c in range(G):
                            nc.tensor.matmul(ps_o[p][32 * c:32 * c + 32, 0:C], he_t[:, j, 32 * c:32 * c + 32],
                                             w2[p][:, c, j, :], start=(j == 0), stop=False, skip_group_check=True)
                    for c in range(G):
                        last = nc.tensor.matmul(ps_o[p][32 * c:32 * c + 32, 0:C], ones[:], b2[p][:, c, :],
                                                start=False, stop=True, skip_group_check=True,
                                                tile_position=(0, 32 * c))
                    last.then_inc(o_done, 1)

                first(0, 0, 0)
                pipelined(pe, NGRP, 2, 2, one)

            @block.gpsimd
            def _(pool):
                def one(g, half, p):
                    if after(g, 2):
                        pool.wait_ge(h_done, g - 1)
                    apart(pool, waits_apart)
                    nc.gpsimd.tensor_copy(xe[p][:], pooled[:, bass.ds(g * G, G), :]).then_inc(xe_ready, 1)

                pipelined(pool, NGRP, 2, 0, one)

            @block.scalar
            def _(act):
                def gelu(g, p):
                    act.wait_ge(h_done, g + 1)
                    if after(g):
                        act.wait_ge(t_done, g)
                    nc.scalar.activation(he[:], ps_h[p][:], ACT.Gelu).then_inc(he_ready, 1)

                def one(g, half, p):
                    if not (isinstance(g, int) and g == NGRP - 1):
                        gelu(g + 1, 1 - p)
                    act.wait_ge(oe_ready, g + 1)
                    if after(g):
                        act.wait_ge(oe_saved, 64 * g)
                    for c in range(G):
                        act.dma_start(d["s_oe"][:, bass.ds(g * G + c, 1), :].rearrange("b e o -> b (e o)"),
                                      oe[p][32 * c:32 * c + 32, :]).then_inc(oe_saved, 16)

                gelu(0, 0)
                pipelined(act, NGRP, 2, 2, one)
                act.wait_ge(oe_saved, 64 * NGRP)

            @block.vector
            def _(dve):
                nc.vector.memset(ones[:], 1.0).then_inc(ones_ready, 1)

                def one(g, half, p):
                    dve.wait_ge(t_done, g + 1)
                    if after(g):
                        dve.wait_ge(o_done, g)
                    nc.vector.tensor_copy(he_t[:], ps_t[:]).then_inc(het_ready, 1)
                    dve.wait_ge(o_done, g + 1)
                    if after(g, 2):
                        dve.wait_ge(oe_saved, 64 * g - 64)
                    nc.vector.tensor_copy(oe[p][:], ps_o[p][:, 0:C]).then_inc(oe_ready, 1)

                pipelined(dve, NGRP, 2, 0, one)


def combine(nc, d, x_sb, out):
    NP = B // 2
    with ExitStack() as ctx:
        st = Store(nc, ctx)
        wn = [st.sb(f"wn_c{i}", [2 * E, L]) for i in range(2)]
        oe = [st.sb(f"oe_c{i}", [2 * E, C]) for i in range(2)]
        ps = [st.ps(f"ps_c{i}", [128, 512]) for i in range(8)]
        in_loaded = [st.sem(f"in_loaded{i}") for i in range(2)]
        mm_done = st.sem("mm_done")
        added = st.sem("added")
        stored = st.sem("stored")

        with nc.Block() as block:
            @block.scalar
            def _(act):
                def one(j, half, jp):
                    if after(j, 2):
                        act.wait_ge(mm_done, 4 * j - 4)
                    act.dma_start(wn[jp][:], d["s_wn"][bass.ds(j, 1)].rearrange("j e l -> (j e) l")
                                  ).then_inc(in_loaded[jp], 16)
                    act.dma_start(oe[jp][:], d["s_oe"][bass.ds(j * 2, 2)].rearrange("b e o -> (b e) o")
                                  ).then_inc(in_loaded[jp], 16)

                pipelined(act, NP, 2, 0, one)

            @block.tensor
            def _(pe):
                def one(j, half, jp):
                    pe.wait_ge(in_loaded[jp], 32 * half + 32)
                    for q in range(2):
                        for h in range(2):
                            k = 2 * q + h
                            if after(j, 2):
                                pe.wait_ge(added, 4 * j + k - 7)
                            nc.tensor.matmul(ps[4 * jp + k][:], oe[jp][E * q:E * q + E, :],
                                             wn[jp][E * q:E * q + E, h * 512:(h + 1) * 512]).then_inc(mm_done, 1)

                pipelined(pe, NP, 2, 0, one)

            @block.vector
            def _(dve):
                def one(j, half, jp):
                    for q in range(2):
                        for h in range(2):
                            k = 2 * q + h
                            dve.wait_ge(mm_done, 4 * j + k + 1)
                            xs = x_sb[:, bass.ds(j * 2 + q, 1), h * 512:(h + 1) * 512].rearrange("c b l -> c (b l)")
                            nc.vector.tensor_tensor(xs, ps[4 * jp + k][:], xs, ALU.add).then_inc(added, 1)

                pipelined(dve, NP, 2, 0, one)

            @block.sync
            def _(sp):
                with sp.Fori(0, B) as b:
                    sp.wait_ge(added, b * 2 + 2)
                    sp.dma_start(out[bass.ds(b, 1)].rearrange("b c l -> c (b l)"),
                                 x_sb[:, bass.ds(b, 1), :].rearrange("c b l -> c (b l)")).then_inc(stored, 16)
                sp.wait_ge(stored, 16 * B)


def build(nc, d, out):
    with ExitStack() as ctx:
        st = Store(nc, ctx)
        x_sb = st.sb("x_sb", [C, B, L])
        with ExitStack() as ctx1:
            s1 = Store(nc, ctx1)
            mask = s1.sb("mask", [Q, NQ, 2 * Q + NG])
            wvo = s1.sb("wvo", [C, C])
            bvo = s1.sb("bvo", [C, C])
            with ExitStack() as ctx2:
                s2 = Store(nc, ctx2)
                ln_r = s2.sb("ln_r", [B, L])
                ln_mr = s2.sb("ln_mr", [B, L])
                spikes = s2.sb("spikes", [B, L])
                scale_cb = s2.sb("scale_cb", [C, B])
                shift_cb = s2.sb("shift_cb", [C, B])
                load_and_norm(nc, d, x_sb, scale_cb, shift_cb)
                rnn_layer(nc, d, x_sb, scale_cb, shift_cb, ln_r, ln_mr, spikes)
                build_mask(nc, d, spikes, ln_r, ln_mr, mask, wvo, bvo)
            attention(nc, d, x_sb, mask, wvo, bvo)
        pooled = st.sb("pooled", [C, E, B])
        route(nc, d, x_sb, pooled)
        experts(nc, d, pooled)
        combine(nc, d, x_sb, out)


def kernel(**inputs):
    import numpy as np
    import concourse.bacc as bacc
    from concourse.bass_utils import run_bass_kernel_spmd

    f = {k: np.asarray(v) for k, v in inputs.items()}

    def rows(w, k):
        return w.reshape(k, 128, -1).transpose(1, 0, 2)

    ch = np.arange(C)
    q, n = np.arange(Q)[:, None], np.arange(Q)[None, :]
    a = {
        "x": f["x"].reshape(B, C, L),
        "L0_conv_gamma": f["L0_conv_gamma"][:, None],
        "L0_conv_beta": f["L0_conv_beta"][:, None],
        "L0_conv_w_in": f["L0_conv_w_in"].T,
        "L0_conv_b_in": f["L0_conv_b_in"].reshape(KI, 128).T,
        "L0_conv_w_ih": rows(f["L0_conv_w_ih"].T, KI),
        "L0_conv_b_ih": f["L0_conv_b_ih"].reshape(KH, 128).T,
        "L0_conv_w_hh": rows(f["L0_conv_w_hh"].T, KH),
        "L0_conv_b_hh": f["L0_conv_b_hh"].reshape(KH, 128).T,
        "L0_conv_w_out": rows(f["L0_conv_w_out"].T, KH),
        "L0_conv_b_out": f["L0_conv_b_out"][:, None],
        "L1_attn_Ws": f["L1_attn_Ws"],
        "L1_attn_bs": f["L1_attn_bs"],
        "L1_attn_Wq": f["L1_attn_Wq"],
        "L1_attn_Wk": f["L1_attn_Wk"],
        "L1_attn_Wv": f["L1_attn_Wv"].T,
        "L1_attn_Wo": f["L1_attn_Wo"],
        "L1_attn_bq": f["L1_attn_bq"][:, None],
        "L1_attn_bk": f["L1_attn_bk"][:, None],
        "L1_attn_bv": f["L1_attn_bv"][:, None],
        "L1_attn_bo": f["L1_attn_bo"][:, None],
        "L1_ffn_gate_w": f["L1_ffn_gate_w"].T,
        "L1_ffn_gate_b": np.concatenate([f["L1_ffn_gate_b"]] * 2)[:, None],
        "w1": f["L1_ffn_weight1"],
        "w2": f["L1_ffn_weight2"],
        "c_group_mean": (ch[:, None] // (C // GROUPS) == ch[None, :] // (C // GROUPS)).astype(np.float32)
        / (C // GROUPS),
        "c_mean": np.full((C, C), 1.0 / C, np.float32),
        "c_ident": np.eye(128, dtype=np.float32),
        "c_tri": np.concatenate([np.where(n >= q, 0.0, NEG), np.where(n <= q, 0.0, NEG)], 1).astype(np.float32),
    }
    nc = bacc.Bacc("TRN2", target_bir_lowering=False, num_devices=1)
    arrays, d = {}, {}
    for name, v in a.items():
        arrays["in_" + name] = np.ascontiguousarray(v)
        d[name] = nc.dram_tensor("in_" + name, v.shape, F32, kind="ExternalInput").ap()
    out = nc.dram_tensor("out_y", (B, C, L), F32, kind="ExternalOutput").ap()
    d["s_ln"] = nc.dram_tensor("s_ln", (2, B, L), F32, kind="Internal").ap()
    d["s_wn"] = nc.dram_tensor("s_wn", (B // 2, 2 * E, L), F32, kind="Internal").ap()
    d["s_oe"] = nc.dram_tensor("s_oe", (B, E, C), F32, kind="Internal").ap()
    build(nc, d, out)
    r = run_bass_kernel_spmd(nc, [arrays], core_ids=[0])
    return r.results[0]["out_y"].reshape(B, C, 32, 32)
```
